# Optimizing a Trainium2 kernel written in Bass

```python
import numpy as np
import jax
import jax.numpy as jnp

def _softmax(x, axis=-1):
    return jax.nn.softmax(x, axis=axis)

def _gelu(x):
    return jax.nn.gelu(x, approximate=True)

def _silu(x):
    return jax.nn.silu(x)

def _sigmoid(x):
    return jax.nn.sigmoid(x)

def _layernorm(x, axis=-1, eps=1e-05):
    m = jnp.mean(x, axis=axis, keepdims=True)
    v = jnp.var(x, axis=axis, keepdims=True)
    return (x - m) / jnp.sqrt(v + eps)

def _scatter_add(tgt, idx, src, axis=0):
    return tgt.at[idx].add(src)

def _segment_sum(src, seg, n):
    return jax.ops.segment_sum(src, seg, n)
kernel_name = 'mk_adaln_d1_jaxref_r8_fc0b66'

def setup_inputs(seed: int=0):
    np.random.seed(seed)
    _w = jnp.asarray

    def _L0_attn_setup():
        import jax, jax.numpy as jnp
        import numpy as np
        B, N, D, F = (4, 512, 128, 64)
        LN_EPS = 1e-05
        ATTN_EPS = 1e-06

        def _layer_norm(x, w, b):
            mu = jnp.mean(x, axis=-1, keepdims=True)
            var = jnp.var(x, axis=-1, keepdims=True)
            return (x - mu) * jax.lax.rsqrt(var + LN_EPS) * w + b

        def _linear(x, w, b):
            return jnp.einsum('bnd,fd->bnf', x, w) + b

        def _causal_linear_attn(Q, K, V, eps=ATTN_EPS):
            b, n, f = K.shape
            d = V.shape[-1]
            Qt = jnp.swapaxes(Q, 0, 1)
            Kt = jnp.swapaxes(K, 0, 1)
            Vt = jnp.swapaxes(V, 0, 1)

            def step(carry, qkv):
                KV, Ks = carry
                q, k, v = qkv
                KV = KV + k[:, :, None] * v[:, None, :]
                Ks = Ks + k
                num = jnp.einsum('bf,bfd->bd', q, KV)
                den = jnp.sum(q * Ks, axis=-1, keepdims=True) + eps
                return ((KV, Ks), num / den)
            init = (jnp.zeros((b, f, d), Q.dtype), jnp.zeros((b, f), Q.dtype))
            _, out = jax.lax.scan(step, init, (Qt, Kt, Vt))
            return jnp.swapaxes(out, 0, 1)
        key = jax.random.key(seed)
        ks = jax.random.split(key, 9)
        s = 0.02
        return {'x': jax.random.normal(ks[0], (B, N, D), dtype=jnp.float32), 'ln1_w': jnp.ones((D,), jnp.float32), 'ln1_b': jnp.zeros((D,), jnp.float32), 'q_w': jax.random.normal(ks[1], (F, D), jnp.float32) * s, 'q_b': jnp.zeros((F,), jnp.float32), 'k_w': jax.random.normal(ks[2], (F, D), jnp.float32) * s, 'k_b': jnp.zeros((F,), jnp.float32), 'v_w': jax.random.normal(ks[3], (D, D), jnp.float32) * s, 'v_b': jnp.zeros((D,), jnp.float32), 'o_w': jax.random.normal(ks[4], (D, D), jnp.float32) * s, 'o_b': jnp.zeros((D,), jnp.float32), 'ln2_w': jnp.ones((D,), jnp.float32), 'ln2_b': jnp.zeros((D,), jnp.float32), 'f1_w': jax.random.normal(ks[5], (4 * D, D), jnp.float32) * s, 'f1_b': jnp.zeros((4 * D,), jnp.float32), 'f2_w': jax.random.normal(ks[6], (D, 4 * D), jnp.float32) * s, 'f2_b': jnp.zeros((D,), jnp.float32)}
    _L0_attn_in = _L0_attn_setup()

    def _L0_ffn_setup():
        import jax, jax.numpy as jnp
        import numpy as np
        DIM = 128
        INTER = 64
        E = 16
        TOPK = 4
        N_GROUPS = 4
        TOPK_GROUPS = 2
        ROUTE_SCALE = 1.0
        INIT_STD = 0.02
        B, S = (2, 128)
        key = jax.random.key(seed)
        ks = jax.random.split(key, 8)
        return {'x': jax.random.normal(ks[0], (B, S, DIM), jnp.float32), 'gate_w': jax.random.normal(ks[1], (E, DIM), jnp.float32) * INIT_STD, 'gate_bias': jnp.zeros((E,), jnp.float32), 'w1': jax.random.normal(ks[2], (E, INTER, DIM), jnp.float32) * INIT_STD, 'w2': jax.random.normal(ks[3], (E, DIM, INTER), jnp.float32) * INIT_STD, 'w3': jax.random.normal(ks[4], (E, INTER, DIM), jnp.float32) * INIT_STD, 'ws1': jax.random.normal(ks[5], (INTER, DIM), jnp.float32) * INIT_STD, 'ws2': jax.random.normal(ks[6], (DIM, INTER), jnp.float32) * INIT_STD, 'ws3': jax.random.normal(ks[7], (INTER, DIM), jnp.float32) * INIT_STD}
    _L0_ffn_in = _L0_ffn_setup()
    _L0_c = _w((lambda *s: np.random.randn(*s).astype(np.float32) * 0.05)(8, 128))
    _L0_wmod = _w((lambda *s: np.random.randn(*s).astype(np.float32) * 0.05)(128, 6 * 128) * 128 ** (-0.5))
    _d = {'L0_attn_x': _L0_attn_in['x'], 'L0_attn_ln1_w': _L0_attn_in['ln1_w'], 'L0_attn_ln1_b': _L0_attn_in['ln1_b'], 'L0_attn_q_w': _L0_attn_in['q_w'], 'L0_attn_q_b': _L0_attn_in['q_b'], 'L0_attn_k_w': _L0_attn_in['k_w'], 'L0_attn_k_b': _L0_attn_in['k_b'], 'L0_attn_v_w': _L0_attn_in['v_w'], 'L0_attn_v_b': _L0_attn_in['v_b'], 'L0_attn_o_w': _L0_attn_in['o_w'], 'L0_attn_o_b': _L0_attn_in['o_b'], 'L0_attn_ln2_w': _L0_attn_in['ln2_w'], 'L0_attn_ln2_b': _L0_attn_in['ln2_b'], 'L0_attn_f1_w': _L0_attn_in['f1_w'], 'L0_attn_f1_b': _L0_attn_in['f1_b'], 'L0_attn_f2_w': _L0_attn_in['f2_w'], 'L0_attn_f2_b': _L0_attn_in['f2_b'], 'L0_ffn_gate_w': _L0_ffn_in['gate_w'], 'L0_ffn_gate_bias': _L0_ffn_in['gate_bias'], 'L0_ffn_w1': _L0_ffn_in['w1'], 'L0_ffn_w2': _L0_ffn_in['w2'], 'L0_ffn_w3': _L0_ffn_in['w3'], 'L0_ffn_ws1': _L0_ffn_in['ws1'], 'L0_ffn_ws2': _L0_ffn_in['ws2'], 'L0_ffn_ws3': _L0_ffn_in['ws3'], 'L0_c': _L0_c, 'L0_wmod': _L0_wmod}
    _x0 = _d['L0_attn_x']
    _d['L0_attn_x'] = jax.random.normal(jax.random.fold_in(jax.random.key(seed), 1), (8, 1024, 128), dtype=_x0.dtype)
    del _x0
    return _d

def reference(L0_attn_x, L0_attn_ln1_w, L0_attn_ln1_b, L0_attn_q_w, L0_attn_q_b, L0_attn_k_w, L0_attn_k_b, L0_attn_v_w, L0_attn_v_b, L0_attn_o_w, L0_attn_o_b, L0_attn_ln2_w, L0_attn_ln2_b, L0_attn_f1_w, L0_attn_f1_b, L0_attn_f2_w, L0_attn_f2_b, L0_ffn_gate_w, L0_ffn_gate_bias, L0_ffn_w1, L0_ffn_w2, L0_ffn_w3, L0_ffn_ws1, L0_ffn_ws2, L0_ffn_ws3, L0_c, L0_wmod):

    def _L0_attn_ref(x, ln1_w, ln1_b, q_w, q_b, k_w, k_b, v_w, v_b, o_w, o_b, ln2_w, ln2_b, f1_w, f1_b, f2_w, f2_b):
        import jax, jax.numpy as jnp
        import numpy as np
        B, N, D, F = (4, 512, 128, 64)
        LN_EPS = 1e-05
        ATTN_EPS = 1e-06

        def _layer_norm(x, w, b):
            mu = jnp.mean(x, axis=-1, keepdims=True)
            var = jnp.var(x, axis=-1, keepdims=True)
            return (x - mu) * jax.lax.rsqrt(var + LN_EPS) * w + b

        def _linear(x, w, b):
            return jnp.einsum('bnd,fd->bnf', x, w) + b

        def _causal_linear_attn(Q, K, V, eps=ATTN_EPS):
            b, n, f = K.shape
            d = V.shape[-1]
            Qt = jnp.swapaxes(Q, 0, 1)
            Kt = jnp.swapaxes(K, 0, 1)
            Vt = jnp.swapaxes(V, 0, 1)

            def step(carry, qkv):
                KV, Ks = carry
                q, k, v = qkv
                KV = KV + k[:, :, None] * v[:, None, :]
                Ks = Ks + k
                num = jnp.einsum('bf,bfd->bd', q, KV)
                den = jnp.sum(q * Ks, axis=-1, keepdims=True) + eps
                return ((KV, Ks), num / den)
            init = (jnp.zeros((b, f, d), Q.dtype), jnp.zeros((b, f), Q.dtype))
            _, out = jax.lax.scan(step, init, (Qt, Kt, Vt))
            return jnp.swapaxes(out, 0, 1)
        x_norm = _layer_norm(x, ln1_w, ln1_b)
        Q = jax.nn.elu(_linear(x_norm, q_w, q_b)) + 1.0
        K = jax.nn.elu(_linear(x_norm, k_w, k_b)) + 1.0
        V = _linear(x_norm, v_w, v_b)
        attn = _causal_linear_attn(Q, K, V)
        attn = _linear(attn, o_w, o_b)
        x = x + attn
        h = _layer_norm(x, ln2_w, ln2_b)
        h = jax.nn.gelu(_linear(h, f1_w, f1_b), approximate=False)
        x = x + _linear(h, f2_w, f2_b)
        return x

    def _L0_ffn_ref(x, gate_w, gate_bias, w1, w2, w3, ws1, ws2, ws3):
        import jax, jax.numpy as jnp
        import numpy as np
        DIM = 128
        INTER = 64
        E = 16
        TOPK = 4
        N_GROUPS = 4
        TOPK_GROUPS = 2
        ROUTE_SCALE = 1.0
        INIT_STD = 0.02
        B, S = (2, 128)
        Bx, Sx, D = x.shape
        T = Bx * Sx
        xf = x.reshape(T, D)
        scores = jax.nn.sigmoid(xf @ gate_w.T)
        original_scores = scores
        s = scores + gate_bias
        sg = s.reshape(T, N_GROUPS, E // N_GROUPS)
        group_scores = sg.max(axis=-1)
        _, gidx = jax.lax.top_k(group_scores, TOPK_GROUPS)
        keep = jnp.zeros((T, N_GROUPS), bool).at[jnp.arange(T)[:, None], gidx].set(True)
        s_masked = jnp.where(keep[:, :, None], sg, -jnp.inf).reshape(T, E)
        _, idx = jax.lax.top_k(s_masked, TOPK)
        weights = jnp.take_along_axis(original_scores, idx, axis=1) * ROUTE_SCALE
        comb = jnp.zeros((T, E), x.dtype).at[jnp.arange(T)[:, None], idx].add(weights)
        h1 = jnp.einsum('td,eid->tei', xf, w1)
        h3 = jnp.einsum('td,eid->tei', xf, w3)
        h = jax.nn.silu(h1) * h3
        y = jnp.einsum('tei,edi,te->td', h, w2, comb)
        z = jax.nn.silu(xf @ ws1.T) * (xf @ ws3.T) @ ws2.T
        return (y + z).reshape(Bx, Sx, D)
    x = L0_attn_x
    mod = (_silu(L0_c) @ L0_wmod).reshape(L0_c.shape[0], 6, 1, -1)
    sa, ca, ga, sb, cb, gb = (mod[:, 0], mod[:, 1], mod[:, 2], mod[:, 3], mod[:, 4], mod[:, 5])
    ga = (2 * (ga >= 0) - 1) * jnp.maximum(jnp.abs(ga), 0.25)
    gb = (2 * (gb >= 0) - 1) * jnp.maximum(jnp.abs(gb), 0.25)
    h = _layernorm(x, axis=-1) * (1 + ca) + sa
    x = x + ga * _L0_attn_ref(h, L0_attn_ln1_w, L0_attn_ln1_b, L0_attn_q_w, L0_attn_q_b, L0_attn_k_w, L0_attn_k_b, L0_attn_v_w, L0_attn_v_b, L0_attn_o_w, L0_attn_o_b, L0_attn_ln2_w, L0_attn_ln2_b, L0_attn_f1_w, L0_attn_f1_b, L0_attn_f2_w, L0_attn_f2_b)
    h = _layernorm(x, axis=-1) * (1 + cb) + sb
    x = x + gb * _L0_ffn_ref(h, L0_ffn_gate_w, L0_ffn_gate_bias, L0_ffn_w1, L0_ffn_w2, L0_ffn_w3, L0_ffn_ws1, L0_ffn_ws2, L0_ffn_ws3)
    return x

_drawn_inputs = setup_inputs


def setup_inputs(seed=0):
    import zlib

    import numpy as np

    out = dict(_drawn_inputs(seed))
    spreads = {'L0_attn_ln1_w': (1.0, 0.6),
     'L0_attn_ln1_b': (0.0, 0.8),
     'L0_attn_q_b': (0.0, 0.8),
     'L0_attn_k_b': (0.0, 2.0),
     'L0_attn_v_b': (0.0, 0.8),
     'L0_attn_o_b': (0.0, 0.31),
     'L0_attn_ln2_w': (1.0, 0.6),
     'L0_attn_ln2_b': (0.0, 0.8),
     'L0_attn_f1_b': (0.0, 0.8),
     'L0_attn_f2_b': (0.0, 0.328),
     'L0_ffn_gate_bias': (0.0, 0.8)}
    factors = {'L0_attn_q_w': 8.0,
     'L0_attn_k_w': 8.0,
     'L0_attn_v_w': 8.0,
     'L0_attn_o_w': 8.0,
     'L0_attn_f1_w': 4.032,
     'L0_attn_f2_w': 3.629,
     'L0_ffn_gate_w': 8.0,
     'L0_ffn_w1': 8.0,
     'L0_ffn_w2': 8.0,
     'L0_ffn_w3': 8.0,
     'L0_ffn_ws1': 8.0,
     'L0_ffn_ws2': 8.0,
     'L0_ffn_ws3': 8.0}
    for name, (base, spread) in spreads.items():
        noise = np.random.default_rng([zlib.crc32(name.encode()), seed]).standard_normal(out[name].shape)
        drawn = base * np.exp(spread * noise) if base else spread * noise
        out[name] = jnp.asarray(drawn.astype(out[name].dtype))
    for name, factor in factors.items():
        out[name] = (out[name] * factor).astype(out[name].dtype)
    return out
```

```python
from contextlib import ExitStack

import concourse.bass as bass
from concourse import mybir

F32 = mybir.dt.float32
F32R = mybir.dt.float32r
BF16 = mybir.dt.bfloat16
ALU = mybir.AluOpType
ACT = mybir.ActivationFunctionType
AX = mybir.AxisListType

P = 128
D = 128
F = 64
NSEQ = 8
STEPS = 8
TILES = 4
W = TILES * P
E = 16
NG = 4
UNITS = 8
ALLU = UNITS + 1
FC = 4
LN_EPS = 1e-5
ATTN_EPS = 1e-6
MASKED = -1e30
SENTINEL = -2e30
CHOSEN = 2e30
GA, SB, CB, GB = range(4)
ROW_SA, ROW_CA, ROW_GA = range(3)


def layer_kernel(nc, a):
    x_v = a["x"].rearrange("(q s t p) d -> q s p t d", q=2, s=STEPS, t=TILES)
    out_v = a["out"].rearrange("(q s t p) d -> q s p t d", q=2, s=STEPS, t=TILES)

    with ExitStack() as ctx:
        def sb(name, shape, dt=F32):
            return ctx.enter_context(nc.sbuf_tensor(name, shape, dt))

        def ps(name, shape):
            return ctx.enter_context(nc.psum_tensor(name, shape, F32))

        def sem(name):
            return ctx.enter_context(nc.semaphore(name))

        ident = sb("ident", [P, P])
        ident_b = sb("ident_b", [P, P], BF16)
        causal = sb("causal", [P, P])
        lower = sb("lower", [P, NG * NG])
        sel = sb("sel", [3 * E, UNITS, P], BF16)
        carry = sb("carry", [P, STEPS])
        vecs = sb("vecs", [P, 8])
        f1b = sb("f1b", [P, FC])
        cT = sb("cT", [P, NSEQ])
        silu_c = sb("silu_c", [P, NSEQ])
        ob_row = sb("ob_row", [P, D])
        gb_row = sb("gb_row", [P, E])
        expo = sb("expo", [P, 2 * TILES])
        eps = sb("eps", [P, 2 * TILES])
        gate_w = sb("gate_w", [P, E])
        modr = sb("modr", [P, 3, NSEQ, D])
        modc = sb("modc", [P, 4, NSEQ])
        gaf2b = sb("gaf2b", [P, NSEQ])
        bq = sb("bq", [P, 2])
        vb_row = sb("vb_row", [P, D])
        f1bias = sb("f1bias", [P, FC])
        wqk_h = sb("wqk_h", [P, 4, P], F32R)
        wqk_l = sb("wqk_l", [P, 4, P], F32R)
        wv_h = sb("wv_h", [P, D], F32R)
        wv_l = sb("wv_l", [P, D], F32R)
        f1_h = sb("f1_h", [P, FC, P], F32R)
        f1_l = sb("f1_l", [P, FC, P], F32R)
        f2_h = sb("f2_h", [P, FC, P], F32R)
        f2_l = sb("f2_l", [P, FC, P], F32R)
        w1_h = sb("w1_h", [P, ALLU, P], F32R)
        w1_l = sb("w1_l", [P, ALLU, P], F32R)
        w3_h = sb("w3_h", [P, UNITS, P], F32R)
        w3_l = sb("w3_l", [P, UNITS, P], F32R)
        w2_h = sb("w2_h", [P, ALLU, P], F32R)
        w2_l = sb("w2_l", [P, ALLU, P], F32R)

        xa = sb("xa", [P, 2, TILES, D])
        xb = sb("xb", [P, 2, TILES, D])
        u = sb("u", [P, 2, TILES, D])
        h = sb("h", [P, 2, TILES, D])
        hb = sb("hb", [P, 2, TILES, D])
        u1 = sb("u1", [P, 2, TILES, D])
        u1T_h = sb("u1T_h", [P, 2, W], F32R)
        u1T_l = sb("u1T_l", [P, 2, W], F32R)
        qT = sb("qT", [P, W])
        kT = sb("kT", [P, W])
        kt = sb("kt", [P, TILES, P])
        v1 = sb("v1", [P, 2, TILES, D + 1])
        scT = sb("scT", [P, 2, P])
        den = sb("den", [P, 2])
        rden = sb("rden", [P, 2])
        state = sb("state", [P, D + 1])
        x1 = sb("x1", [P, 2, TILES, D])
        un = sb("un", [P, 2, TILES, D])
        u2T_h = sb("u2T_h", [P, 2, W], F32R)
        u2T_l = sb("u2T_l", [P, 2, W], F32R)
        gf = sb("gf", [P, 2, W])
        ghi = sb("ghi", [P, 3, W], F32R)
        glo = sb("glo", [P, 3, W], F32R)
        y2 = sb("y2", [P, 2, W])
        xg = sb("xg", [P, 2, TILES, D])
        X = sb("X", [P, 2, TILES, D])
        Xo = sb("Xo", [P, 2, TILES, D])
        h2T = sb("h2T", [P, 2, W])
        h2_h = sb("h2_h", [P, 2, W], F32R)
        h2_l = sb("h2_l", [P, 2, W], F32R)
        combT = sb("combT", [3 * E, 2 * W], BF16)
        stats = {n: sb(f"st_{n}", [P, 8, 6]) for n in ("x", "h", "x1", "X")}
        mv = {n: sb(f"mv_{n}", [P, 8, 2]) for n in stats}
        ve = {n: sb(f"ve_{n}", [P, 8]) for n in stats}
        rstd = {n: sb(f"rstd_{n}", [P, 8]) for n in stats}
        th = sb("th", [P, 8, E])
        score = sb("score", [P, 8, E])
        biased = sb("biased", [P, 8, E])
        gmax = sb("gmax", [P, 8 * NG])
        gt = sb("gt", [P, 8, NG, NG])
        ge = sb("ge", [P, 8, NG, NG])
        rank = sb("rank", [P, 8 * NG])
        penalty = sb("penalty", [P, 8, NG])
        cand = sb("cand", [P, 8, E + 4])
        top = sb("top", [P, 8, 8])
        marked = sb("marked", [P, 8, E + 4])
        comb = sb("comb", [P, 8, E])
        rest = sb("rest", [P, 8, E])
        parts = sb("parts", [P, 8, 3 * E], BF16)
        g = sb("g", [P, 2, W])
        gu = sb("gu", [P, 2, W])
        hid = sb("hid", [P, 3, W])
        hid_h = sb("hid_h", [P, 3, W], F32R)
        hid_l = sb("hid_l", [P, 3, W], F32R)
        y = sb("y", [P, W])
        o = sb("o", [P, 2, TILES, D])
        eQ, eK = u1[:, 0, :, :], u1[:, 1, :, :]
        rQ, rK = y2[:, 0, :], y2[:, 1, :]

        psA, psB, psC, psY = ps("psA", [P, W]), ps("psB", [P, W]), ps("psC", [P, W]), ps("psY", [P, W])
        psR = ps("psR", [P, 2, W])
        psP = ps("psP", [P, 2, W])
        banks = [psA[:, :], psB[:, :], psC[:, :], psY[:, :], psR[:, 0, :], psR[:, 1, :], psP[:, 0, :], psP[:, 1, :]]
        NUM, KV = P, 2 * P + 4

        small_in, attn_in, moe_in = sem("small_in"), sem("attn_in"), sem("moe_in")
        s_silu, s_cb, s_modr_ps, s_modr_cp, s_modc_ps, s_setup = (
            sem(n) for n in ("c_silu", "c_spread", "modr_ps", "modr_copied", "modc_ps", "setup_step"))
        s_fold_ps, s_wvo, s_vb_ps, s_modr, s_weights, s_pool0 = (
            sem(n) for n in ("fold_ps", "wvo_ready", "vbias_ps", "modr_ready", "weights_ready", "pool_consts"))
        xa_in = [sem("xa_in0"), sem("xa_in1")]
        xb_in = [sem("xb_in0"), sem("xb_in1")]
        stored = [sem("stored0"), sem("stored1")]
        st_done = {n: sem(f"stats_{n}") for n in stats}
        mv_done = {n: sem(f"mean_var_{n}") for n in stats}
        ve_done = {n: sem(f"var_eps_{n}") for n in stats}
        rstd_done = {n: sem(f"rstd_{n}") for n in stats}
        names = """u_ready u_scaled h_ready hb_ready u1_ready u1T_ps u1hi u1lo q_ps k_ps q_exp k_exp qT_ready
            kT_ready v_ps v_ready kt_ps kt_ready sc_ps sc_ready num_ps den_ready rden_ready x1_ready state_sum
            state_ready u2_ready u2T_ps u2hi u2lo x1_gated xg_ready f1_ps gelu_done g_hi g_lo f2_ps y2_ready
            y2T_ps X_ready Xo_ready u3_ready u3T_ps h2_ready h2hi h2lo gate_ps tanh_done route parts_ready
            parts_ps combT_ready w1_ps w3_ps comb_ps silu_done gu_ready hid_ready hid_hi hid_lo w2_ps y_ready
            yT_ps out_ready""".split()
        S = {n: sem(n) for n in names}
        (u_ready, u_scaled, h_ready, hb_ready, u1_ready, u1T_ps, u1hi, u1lo, q_ps, k_ps, q_exp, k_exp, qT_ready,
         kT_ready, v_ps, v_ready, kt_ps, kt_ready, sc_ps, sc_ready, num_ps, den_ready, rden_ready, x1_ready, state_sum,
         state_ready, u2_ready, u2T_ps, u2hi, u2lo, x1_gated, xg_ready, f1_ps, gelu_done, g_hi, g_lo, f2_ps, y2_ready,
         y2T_ps, X_ready, Xo_ready, u3_ready, u3T_ps, h2_ready, h2hi, h2lo, gate_ps, tanh_done, route, parts_ready,
         parts_ps, combT_ready, w1_ps, w3_ps, comb_ps, silu_done, gu_ready, hid_ready, hid_hi, hid_lo, w2_ps, y_ready,
         yT_ps, out_ready) = (S[n] for n in names)

        ROUTE = 17

        def iterations(eng, iteration):
            iteration(None, 0, 1, 2)
            with eng.Fori(1, STEPS - 2) as t:
                iteration(t - 1, t, t + 1, t + 2)
            iteration(STEPS - 3, STEPS - 2, STEPS - 1, None)
            iteration(STEPS - 2, STEPS - 1, None, None)
            iteration(STEPS - 1, None, None, None)

        wait_value = {e.engine: e.alloc_register("wait_value") for e in (nc.sync, nc.tensor, nc.vector)}

        def stand_alone(eng, semaphore, value):
            if not isinstance(value, int):
                eng.reg_mov(wait_value[eng.engine], value)
                value = wait_value[eng.engine]
            eng.wait_ge(small_in, 16 * len(SMALL))
            eng.wait_ge(semaphore, value)

        def seq(s, q):
            return s // 2 + NSEQ // 2 * q

        def wide(row, n=TILES):
            return row.unsqueeze(1).to_broadcast([P, n, row.shape[-1]])

        raw_w1, raw_w3, raw_w2 = X, Xo, h2T
        raw_f1, raw_f2 = g, gu
        raw_sh = hid
        raw_qk = y
        raw_v = o
        wmod = xg
        raw_vw, raw_owT = o[:, 0, 0, :], o[:, 0, 1, :]
        wvo = o[:, 0, 2, :]
        ln1b_sp, vb_sp = o[:, 1, 0, :], o[:, 1, 1, :]
        LN1W, LN1B, LN2W, LN2B, QB, KB, VB, F2B = range(8)
        cspread = x1
        flat = lambda t3: t3[:, :, :, :].rearrange("p a b c -> p (a b c)")

        SMALL = [(cT[:, :], "cT"), (flat(wmod)[:, 0:6 * D], "wmod"), (vecs[:, :], "vecs"), (f1b[:, :], "f1b")]
        ATTN = [(raw_vw, "v_w"), (raw_owT, "o_wT"), (raw_qk[:, :], "qk_wT"), (ident[:, :], "ident"),
                (causal[:, :], "causal"), (carry[:, :], "carry"), (raw_f1[:, 0, :], "f1_wT"),
                (ob_row[:, :], "o_b_row"), (gb_row[:, :], "gate_b_row")]
        MOE = [(flat(raw_w1), "w1T"), (flat(raw_w3), "w3T"), (raw_w2[:, :, :].rearrange("p a b -> p (a b)"), "w2T"),
               (raw_sh[:, 0, 0:P], "ws13T"), (raw_sh[F:P, 1, 0:P], "ws2T"), (raw_f2[:, 0, :], "f2_wT"),
               (gate_w[:, :], "gate_wT"), (ident_b[:, :], "ident_b"), (lower[:, :], "lower"),
               (sel[:, :, :].rearrange("k u m -> k (u m)"), "sel")]

        block = ctx.enter_context(nc.Block())

        @block.sync
        def _(sp):
            def rows_of(view, q, s):
                return view[q, bass.ds(s, 1), :, :, :].rearrange("o p t d -> (o p) t d")

            def load_x(dst, loaded, s):
                for q in range(2):
                    sp.dma_start(dst[:, q, :, :], rows_of(x_v, q, s)).then_inc(loaded[q], 16)

            def get(places, done):
                for dst, name in places:
                    sp.dma_start(dst, a[name]).then_inc(done, 16)

            get(SMALL, small_in)
            load_x(xa, xa_in, 0)
            get(ATTN, attn_in)
            get(MOE, moe_in)
            sp.wait_ge(u_ready, 2)
            load_x(xa, xa_in, 1)

            def iteration(c, s, p, m):
                if m is not None:
                    stand_alone(sp, u_ready, 2 * m)
                    load_x(xa, xa_in, m)
                if s is not None:
                    if not (isinstance(s, int) and s == 0):
                        stand_alone(sp, xg_ready, 2 * s)
                    load_x(xb, xb_in, s)
                if c is not None:
                    for q in range(2):
                        stand_alone(sp, out_ready, 2 * c + q + 1)
                        sp.dma_start(rows_of(out_v, q, c), o[:, q, :, :]).then_inc(stored[q], 16)
                if s is not None:
                    sp.wait_ge(X_ready, 2 * s + 2)
                    sp.dma_start(Xo[:, :, :, :], X[:, :, :, :]).then_inc(Xo_ready, 16)
                if c is not None:
                    for q in range(2):
                        stand_alone(sp, stored[q], 16 * c + 16)

            iterations(sp, iteration)

        @block.tensor
        def _(pe):
            def product(out, w_h, w_l, x_h, x_l, start=True, stop=True):
                pe.matmul(out, w_h, x_h, start=start, stop=False)
                pe.matmul(out, w_l, x_h, start=False, stop=False)
                return pe.matmul(out, w_h, x_l, start=False, stop=stop)

            pe.wait_ge(small_in, 16 * len(SMALL))
            pe.wait_ge(s_cb, 1)
            wm = flat(wmod)
            for b in range(NSEQ):
                pe.matmul(banks[b][:, 0:3 * D], cspread[:, b // TILES, b % TILES, :], wm[:, 0:3 * D],
                          start=True, stop=True).then_inc(s_modr_ps, 1)
            pe.wait_ge(s_modr_cp, NSEQ)
            for j in range(4):
                last = pe.matmul(psA[:, j * NSEQ:(j + 1) * NSEQ], wm[:, (2 + j) * D:(3 + j) * D], silu_c[:, :],
                                 start=True, stop=True)
            last.then_inc(s_modc_ps, 1)
            pe.wait_ge(attn_in, 16 * len(ATTN))
            pe.matmul(psB[:, 0:D], raw_vw, raw_owT, start=True, stop=True)
            for k in range(2):
                for q in range(2):
                    pe.matmul(psC[:, k:k + 1], raw_qk[:, (2 * k + q) * P:(2 * k + q + 1) * P], vecs[:, LN1B:LN1B + 1],
                              start=(q == 0), stop=(q == 1))
            for c in range(FC):
                last = pe.matmul(psY[:, c:c + 1], raw_f1[:, 0, c * P:(c + 1) * P], vecs[:, LN2B:LN2B + 1],
                                 start=True, stop=True)
            last.then_inc(s_fold_ps, 1)
            pe.wait_ge(s_wvo, 1)
            pe.matmul(psR[:, 0, 0:D], ln1b_sp, wvo, start=True, stop=False)
            pe.matmul(psR[:, 0, 0:D], vb_sp, raw_owT, start=False, stop=True).then_inc(s_vb_ps, 1)

            def transposes(bank, src, done):
                for t in range(TILES):
                    last = pe.transpose(bank[:, t * P:(t + 1) * P], src[:, t, :], ident[:, :])
                last.then_inc(done, 1)

            def p_transpose(p, q):
                pe.wait_ge(u1_ready, 2 * p + q + 1)
                if q == 0 and not (isinstance(p, int) and p == 0):
                    pe.wait_ge(kt_ready, p)
                if q == 1 and not (isinstance(p, int) and p == 0):
                    pe.wait_ge(k_exp, p)
                transposes(psP[:, q, :], u1[:, q, :, :], u1T_ps)

            def p_v(p, q):
                pe.wait_ge(u1hi, 2 * p + q + 1)
                pe.wait_ge(u1lo, 2 * p + q + 1)
                for t in range(TILES):
                    cols = slice(t * P, (t + 1) * P)
                    last = product(psP[:, q, cols], u1T_h[:, q, cols], u1T_l[:, q, cols], wv_h[:, :], wv_l[:, :])
                last.then_inc(v_ps, 1)

            def p_qk(p, k):
                pe.wait_ge(v_ready, 2 * p + k + 1)
                for q in range(2):
                    last = product(psP[:, k, :], wqk_h[:, 2 * k + q, :], wqk_l[:, 2 * k + q, :],
                                   u1T_h[:, q, :], u1T_l[:, q, :], start=(q == 0), stop=(q == 1))
                last.then_inc(k_ps if k else q_ps, 1)

            def p_kt(p):
                pe.wait_ge(q_exp, p + 1)
                pe.wait_ge(kT_ready, p + 1)
                for t in range(TILES):
                    last = pe.transpose(psP[:, 0, t * P:(t + 1) * P], kT[:, t * P:(t + 1) * P], ident[:, :])
                last.then_inc(kt_ps, 1)

            def a_scores(s, t):
                if t == 0:
                    pe.wait_ge(qT_ready, s + 1)
                    pe.wait_ge(kT_ready, s + 1)
                    if not (isinstance(s, int) and s == 0):
                        pe.wait_ge(tanh_done, s)
                        pe.wait_ge(combT_ready, s)
                else:
                    pe.wait_ge(x1_ready, TILES * s + t)
                cols = slice(t * P, (t + 1) * P)
                for q in range(2):
                    rows = slice(F * q, F * q + F)
                    last = pe.matmul(psR[:, q, 0:P], kT[rows, cols], qT[rows, cols], start=True, stop=True)
                last.then_inc(sc_ps, 1)

            def a_sums(s, t):
                if t == 0:
                    pe.wait_ge(kt_ready, s + 1)
                    pe.wait_ge(v_ready, 2 * s + 2)
                    pe.wait_ge(state_ready, s + 1)
                pe.wait_ge(sc_ready, TILES * s + t + 1)
                cols = slice(t * P, (t + 1) * P)
                for q in range(2):
                    rows = slice(F * q, F * q + F)
                    num = psR[:, q, NUM:NUM + D + 1]
                    pe.matmul(num, scT[:, q, :], v1[:, q, t, :], start=True, stop=False)
                    pe.matmul(num, qT[rows, cols], state[rows, :], start=False, stop=True)
                    last = pe.matmul(psR[rows, q, KV:KV + D + 1], kt[:, t, rows], v1[:, q, t, :], start=True, stop=True)
                last.then_inc(num_ps, 1)

            def a_transpose2(s, q):
                pe.wait_ge(u2_ready, 2 * s + q + 1)
                transposes(psR[:, q, :], un[:, q, :, :], u2T_ps)

            def a_f1(c, s, i):
                q, j = i // FC, i % FC
                if j == 0:
                    pe.wait_ge(u2hi, 2 * s + q + 1)
                    pe.wait_ge(u2lo, 2 * s + q + 1)
                if c is not None and i == 0:
                    pe.wait_ge(hid_ready, 2 * ALLU * c + ALLU)
                if c is not None and i == 1:
                    pe.wait_ge(gu_ready, 2 * UNITS * c + UNITS)
                if i >= 2:
                    pe.wait_ge(gelu_done, 2 * FC * s + i - 1)
                product((psA, psB)[i % 2][:, :], f1_h[:, j, :], f1_l[:, j, :], u2T_h[:, q, :],
                        u2T_l[:, q, :]).then_inc(f1_ps, 1)

            def a_f2(s, i):
                q, j = i // FC, i % FC
                pe.wait_ge(g_hi, 2 * FC * s + i + 1)
                pe.wait_ge(g_lo, 2 * FC * s + i + 1)
                product(psR[:, q, :], f2_h[:, j, :], f2_l[:, j, :], ghi[:, i % 3, :], glo[:, i % 3, :],
                        start=(j == 0), stop=(j == FC - 1)).then_inc(f2_ps, 1)

            def a_y2T(s, q):
                pe.wait_ge(y2_ready, 2 * s + q + 1)
                for t in range(TILES):
                    last = pe.transpose(psR[:, q, t * P:(t + 1) * P], y2[:, q, t * P:(t + 1) * P], ident[:, :])
                last.then_inc(y2T_ps, 1)

            def a_transpose3(s, q):
                pe.wait_ge(u3_ready, 2 * s + q + 1)
                transposes(psR[:, q, :], un[:, q, :, :], u3T_ps)

            def a_gate(s):
                pe.wait_ge(h2_ready, 2 * s + 2)
                for k in range(8):
                    last = pe.matmul(psR[:, 0, k * E:(k + 1) * E], h2T[:, k // TILES, (k % TILES) * P:(k % TILES + 1) * P],
                                     gate_w[:, :], start=True, stop=True)
                last.then_inc(gate_ps, 1)

            def a_parts(s):
                stand_alone(pe, parts_ready, s + 1)
                wb = psR[:, 1, :].bitcast(BF16)
                for k in range(8):
                    last = pe.transpose(wb[0:3 * E, k * P:(k + 1) * P], parts[:, k, :], ident_b[:, :])
                last.then_inc(parts_ps, 1)

            def c_up(c, n, s):
                q, uu = n // ALLU, n % ALLU
                if uu == 0:
                    pe.wait_ge(h2hi, 2 * c + q + 1)
                    pe.wait_ge(h2lo, 2 * c + q + 1)
                    if q == 1 and s is not None:
                        pe.wait_ge(gelu_done, 2 * FC * s + 2 * FC)
                if n:
                    if uu == 0:
                        pe.wait_ge(hid_ready, 2 * ALLU * c + n)
                    else:
                        pe.wait_ge(silu_done, 2 * ALLU * c + n)
                product(psA[:, :], w1_h[:, uu, :], w1_l[:, uu, :], h2_h[:, q, :], h2_l[:, q, :]).then_inc(w1_ps, 1)
                if uu < UNITS:
                    if n:
                        pe.wait_ge(gu_ready, 2 * UNITS * c + UNITS * q + uu)
                    product(psB[:, :], w3_h[:, uu, :], w3_l[:, uu, :], h2_h[:, q, :], h2_l[:, q, :]).then_inc(w3_ps, 1)

            def c_comb(c, n):
                q, uu = n // ALLU, n % ALLU
                if uu == UNITS:
                    return
                if n == 0:
                    pe.wait_ge(combT_ready, c + 1)
                if n:
                    pe.wait_ge(hid_ready, 2 * ALLU * c + n)
                pe.matmul(psC[:, :], sel[:, uu, :], combT[:, q * W:(q + 1) * W], start=True, stop=True).then_inc(comb_ps, 1)

            def c_down(c, n):
                q, uu = n // ALLU, n % ALLU
                pe.wait_ge(hid_hi, 2 * ALLU * c + n + 1)
                pe.wait_ge(hid_lo, 2 * ALLU * c + n + 1)
                if n == ALLU:
                    pe.wait_ge(y_ready, 2 * c + 1)
                rows = slice(0, P) if uu < UNITS else slice(F, P)
                product(psY[:, :], w2_h[rows, uu, :], w2_l[rows, uu, :], hid_h[rows, n % 3, :], hid_l[rows, n % 3, :],
                        start=(uu == 0), stop=(uu == UNITS)).then_inc(w2_ps, 1)

            def c_yT(c, q):
                pe.wait_ge(y_ready, 2 * c + q + 1)
                if q == 0:
                    pe.wait_ge(k_exp, min(c + 3, STEPS) if isinstance(c, int) else c + 3)
                else:
                    pe.wait_ge(out_ready, 2 * c + 1)
                for t in range(TILES):
                    last = pe.transpose(psP[:, 1, t * P:(t + 1) * P], y[:, t * P:(t + 1) * P], ident[:, :])
                last.then_inc(yT_ps, 1)

            pe.wait_ge(s_weights, 1)
            for q in range(2):
                p_transpose(0, q)
            for q in range(2):
                p_v(0, q)
            for k in range(2):
                p_qk(0, k)
            p_kt(0)
            pe.wait_ge(s_weights, 2)
            pe.wait_ge(moe_in, 16 * len(MOE))

            def iteration(c, s, p, m):
                for n in range(2 * ALLU + 2):
                    if n == ALLU:
                        if s is not None:
                            for i in range(2 * FC + 2):
                                if i < 2 * FC:
                                    a_f1(c, s, i)
                                if i >= 2:
                                    a_f2(s, i - 2)
                    if c is not None and n < 2 * ALLU:
                        c_up(c, n, s)
                    if s is not None and n < TILES:
                        a_scores(s, n)
                    if c is not None and n < 2 * ALLU:
                        c_comb(c, n)
                    if c is not None and n >= 2:
                        c_down(c, n - 2)
                    if s is not None and n < TILES:
                        a_sums(s, n)
                    if p is not None and n == 4:
                        p_transpose(p, 0)
                        p_transpose(p, 1)
                    if p is not None and n == 6:
                        p_v(p, 0)
                        p_v(p, 1)
                    if s is not None and n == 7:
                        a_transpose2(s, 0)
                        a_transpose2(s, 1)
                    if p is not None and n == 8:
                        p_qk(p, 0)
                        p_qk(p, 1)
                    if s is not None and n == 9:
                        a_y2T(s, 0)
                        a_y2T(s, 1)
                    if p is not None and n == 10:
                        p_kt(p)
                    if c is not None and n == 12:
                        c_yT(c, 0)
                    if s is not None and n == 14:
                        a_transpose3(s, 0)
                        a_transpose3(s, 1)
                    if s is not None and n == 15:
                        a_gate(s)
                    if s is not None and n == 19:
                        a_parts(s)
                if c is not None:
                    c_yT(c, 1)

            iterations(pe, iteration)

        @block.scalar
        def _(act):
            act.wait_ge(small_in, 16 * len(SMALL))
            act.activation(silu_c[:, :], cT[:, :], ACT.Silu).then_inc(s_silu, 1)

            def p_u1hi(p, q):
                act.wait_ge(u1T_ps, 2 * p + q + 1)
                act.activation(u1T_h[:, q, :], psP[:, q, :], ACT.Copy).then_inc(u1hi, 1)

            def p_exps(p):
                for k in range(2):
                    act.wait_ge(k_ps if k else q_ps, p + 1)
                    act.activation((eQ, eK)[k].rearrange("p t d -> p (t d)"), psP[:, k, :], ACT.Exp, bias=bq[:, k:k + 1])
                    act.activation((rQ, rK)[k], psP[:, k, :], ACT.Relu, bias=bq[:, k:k + 1]).then_inc(k_exp if k else q_exp, 1)

            def p_kt(p):
                act.wait_ge(kt_ps, p + 1)
                act.activation(kt[:, :, :].rearrange("p t d -> p (t d)"), psP[:, 0, :], ACT.Copy).then_inc(kt_ready, 1)

            def a_u2hi(s, q):
                act.wait_ge(u2T_ps, 2 * s + q + 1)
                act.activation(u2T_h[:, q, :], psR[:, q, :], ACT.Copy).then_inc(u2hi, 1)

            def a_gelu(s, i):
                act.wait_ge(f1_ps, 2 * FC * s + i + 1)
                if i >= 2:
                    act.wait_ge(g_hi, 2 * FC * s + i - 1)
                    act.wait_ge(g_lo, 2 * FC * s + i - 1)
                act.activation(gf[:, i % 2, :], (psA, psB)[i % 2][:, :], ACT.Gelu,
                               bias=f1bias[:, i % FC:i % FC + 1]).then_inc(gelu_done, 1)

            def a_y2(s, q):
                act.wait_ge(f2_ps, 2 * FC * s + FC * q + FC)
                b = seq(s, q)
                act.activation(y2[:, q, :], psR[:, q, :], ACT.Identity, scale=modc[:, GA, bass.ds(b, 1)],
                               bias=gaf2b[:, bass.ds(b, 1)]).then_inc(y2_ready, 1)

            def a_h2(s, q):
                act.wait_ge(u3T_ps, 2 * s + q + 1)
                b = seq(s, q)
                act.activation(h2T[:, q, :], psR[:, q, :], ACT.Identity, scale=modc[:, CB, bass.ds(b, 1)],
                               bias=modc[:, SB, bass.ds(b, 1)]).then_inc(h2_ready, 1)

            def a_tanh(s):
                act.wait_ge(gate_ps, s + 1)
                act.activation(th[:, :, :].rearrange("p k e -> p (k e)"), psR[:, 0, 0:8 * E], ACT.Tanh,
                               scale=0.5).then_inc(tanh_done, 1)

            def a_combT(s):
                act.wait_ge(parts_ps, s + 1)
                act.activation(combT[:, :], psR[0:3 * E, 1, :].bitcast(BF16), ACT.Copy).then_inc(combT_ready, 1)

            def c_silu(c, n):
                uu = n % ALLU
                act.wait_ge(w1_ps, 2 * ALLU * c + n + 1)
                if uu < UNITS:
                    act.activation(g[:, n % 2, :], psA[:, :], ACT.Silu).then_inc(silu_done, 1)
                else:
                    act.activation(g[F:P, n % 2, :], psA[0:F, :], ACT.Silu).then_inc(silu_done, 1)

            def c_hi(c, n):
                act.wait_ge(hid_ready, 2 * ALLU * c + n + 1)
                rows = slice(0, P) if n % ALLU < UNITS else slice(F, P)
                act.activation(hid_h[rows, n % 3, :], hid[rows, n % 3, :], ACT.Copy).then_inc(hid_hi, 1)

            def c_y(c, q):
                act.wait_ge(w2_ps, 2 * ALLU * c + ALLU * q + ALLU)
                act.activation(y[:, :], psY[:, :], ACT.Copy,
                               scale=modc[:, GB, bass.ds(seq(c, q), 1)]).then_inc(y_ready, 1)

            act.wait_ge(s_weights, 1)
            for q in range(2):
                p_u1hi(0, q)
            p_exps(0)
            p_kt(0)
            act.wait_ge(s_weights, 2)

            def iteration(c, s, p, m):
                for n in range(2 * ALLU + 2):
                    if n == ALLU and s is not None:
                        if c is not None:
                            c_hi(c, n - 1)
                        for i in range(2 * FC):
                            a_gelu(s, i)
                            if i == 6:
                                a_y2(s, 0)
                        a_y2(s, 1)
                        if p is not None:
                            act.wait_ge(y2T_ps, 2 * s + 2)
                            p_exps(p)
                    elif c is not None and 1 <= n <= 2 * ALLU:
                        c_hi(c, n - 1)
                    if c is not None and n == ALLU + 2:
                        c_y(c, 0)
                    if c is not None and n < 2 * ALLU:
                        c_silu(c, n)
                    if p is not None and n == 5:
                        p_u1hi(p, 0)
                        p_u1hi(p, 1)
                    if s is not None and n == 8:
                        a_u2hi(s, 0)
                        a_u2hi(s, 1)
                    if p is not None and n == 10:
                        p_kt(p)
                    if s is not None and n == 14:
                        a_h2(s, 0)
                        a_h2(s, 1)
                    if s is not None and n == 15:
                        a_tanh(s)
                    if s is not None and n == 19:
                        a_combT(s)
                if c is not None:
                    c_y(c, 1)

            iterations(act, iteration)

        @block.gpsimd
        def _(pool):
            pool.memset(expo[:, :], -0.5).then_inc(s_pool0, 1)
            pool.memset(eps[:, :], LN_EPS).then_inc(s_pool0, 1)
            pool.wait_ge(s_pool0, 2)

            def inv_std(name, s):
                pool.wait_ge(mv_done[name], s + 1)
                pool.tensor_tensor(ve[name][:, :], mv[name][:, :, 1], eps[:, :], ALU.add).then_inc(ve_done[name], 1)
                pool.wait_ge(ve_done[name], s + 1)
                pool.tensor_tensor(rstd[name][:, :], ve[name][:, :], expo[:, :], ALU.pow).then_inc(rstd_done[name], 1)

            def modrow(r, s, q):
                row = modr[:, r, bass.ds(seq(s, q), 1), :]
                return row.to_broadcast([P, TILES, D])

            def m_affine(m, q):
                pool.wait_ge(u_ready, 2 * m + q + 1)
                pool.tensor_tensor(u[:, q, :, :], u[:, q, :, :], modrow(ROW_CA, m, q), ALU.mult).then_inc(u_scaled, 1)
                pool.wait_ge(u_scaled, 2 * m + q + 1)
                pool.tensor_tensor(h[:, q, :, :], u[:, q, :, :], modrow(ROW_SA, m, q), ALU.add).then_inc(h_ready, 1)

            def p_hb(s, p, q):
                if s is not None:
                    pool.wait_ge(x1_ready, TILES * s + TILES)
                pool.tensor_tensor(hb[:, q, :, :], h[:, q, :, :], wide(ob_row[:, :]), ALU.add).then_inc(hb_ready, 1)

            def a_mix(s, q):
                pool.wait_ge(x1_ready, TILES * s + TILES)
                pool.tensor_tensor(xg[:, q, :, :], x1[:, q, :, :], modrow(ROW_GA, s, q), ALU.mult).then_inc(x1_gated, 1)
                pool.wait_ge(x1_gated, 2 * s + q + 1)
                pool.wait_ge(xb_in[q], 16 * s + 16)
                pool.tensor_tensor(xg[:, q, :, :], xg[:, q, :, :], xb[:, q, :, :], ALU.add).then_inc(xg_ready, 1)

            def a_glo(s, i):
                pool.wait_ge(g_hi, 2 * FC * s + i + 1)
                pool.tensor_tensor(glo[:, i % 3, :], gf[:, i % 2, :], ghi[:, i % 3, :].bitcast(F32),
                                   ALU.subtract).then_inc(g_lo, 1)

            def a_h2lo(s, q):
                pool.wait_ge(h2hi, 2 * s + q + 1)
                pool.tensor_tensor(h2_l[:, q, :], h2T[:, q, :], h2_h[:, q, :].bitcast(F32), ALU.subtract).then_inc(h2lo, 1)

            def c_lo(c, n):
                pool.wait_ge(hid_hi, 2 * ALLU * c + n + 1)
                pool.tensor_tensor(hid_l[:, n % 3, :], hid[:, n % 3, :], hid_h[:, n % 3, :].bitcast(F32),
                                   ALU.subtract).then_inc(hid_lo, 1)

            inv_std("x", 0)
            pool.wait_ge(s_modr, 1)
            for q in range(2):
                m_affine(0, q)
            inv_std("h", 0)
            for q in range(2):
                p_hb(None, 0, q)
            inv_std("x", 1)
            pool.wait_ge(u1_ready, 2)
            for q in range(2):
                m_affine(1, q)

            def iteration(c, s, p, m):
                for n in range(2 * ALLU + 2):
                    if n == ALLU and s is not None:
                        if c is not None:
                            c_lo(c, n - 1)
                        for i in range(2 * FC):
                            a_glo(s, i)
                    elif c is not None and 1 <= n <= 2 * ALLU:
                        c_lo(c, n - 1)
                    if p is not None and n == 1:
                        inv_std("h", p)
                    if s is not None and n == 4:
                        inv_std("x1", s)
                    if p is not None and n == 5:
                        p_hb(s, p, 0)
                        p_hb(s, p, 1)
                    if s is not None and n == 6:
                        a_mix(s, 0)
                    if s is not None and n == 7:
                        a_mix(s, 1)
                    if m is not None and n == 11:
                        inv_std("x", m)
                    if s is not None and n == 12:
                        inv_std("X", s)
                    if m is not None and n == 14:
                        m_affine(m, 0)
                    if m is not None and n == 16:
                        m_affine(m, 1)
                    if s is not None and n == 17:
                        a_h2lo(s, 0)
                    if s is not None and n == 19:
                        a_h2lo(s, 1)

            iterations(pool, iteration)

        @block.vector
        def _(dve):
            link = [0]

            def chain(ins):
                link[0] += 1
                ins.then_inc(s_setup, 1)
                dve.wait_ge(s_setup, link[0])

            def bn(name, src, k):
                return dve.bn_stats(stats[name][:, k, :], src)

            def aggregate(name, s):
                stand_alone(dve, st_done[name], s + 1)
                for k in range(8):
                    last = dve.bn_aggr(mv[name][:, k, :], stats[name][:, k, :])
                last.then_inc(mv_done[name], 1)

            def normalise(dst, src, name, q):
                for t in range(TILES):
                    k = q * TILES + t
                    last = dve.tensor_scalar(dst[:, q, t, :], src[:, q, t, :], mv[name][:, k, 0:1],
                                             rstd[name][:, k:k + 1], ALU.subtract, ALU.mult)
                return last

            def m_stats(m):
                for q in range(2):
                    dve.wait_ge(xa_in[q], 16 * m + 16)
                    for t in range(TILES):
                        last = bn("x", xa[:, q, t, :], q * TILES + t)
                last.then_inc(st_done["x"], 1)
                aggregate("x", m)

            def m_norm(m):
                dve.wait_ge(rstd_done["x"], m + 1)
                for q in range(2):
                    normalise(u, xa, "x", q).then_inc(u_ready, 1)

            def p_stats(p):
                dve.wait_ge(h_ready, 2 * p + 2)
                for k in range(8):
                    last = bn("h", h[:, k // TILES, k % TILES, :], k)
                last.then_inc(st_done["h"], 1)
                aggregate("h", p)

            def p_norm(p):
                dve.wait_ge(rstd_done["h"], p + 1)
                if not (isinstance(p, int) and p == 0):
                    dve.wait_ge(kT_ready, p)
                for q in range(2):
                    normalise(u1, h, "h", q).then_inc(u1_ready, 1)

            def p_u1lo(p, q):
                dve.wait_ge(u1hi, 2 * p + q + 1)
                dve.tensor_tensor(u1T_l[:, q, :], psP[:, q, :], u1T_h[:, q, :].bitcast(F32), ALU.subtract).then_inc(u1lo, 1)

            def p_v(p, q):
                dve.wait_ge(v_ps, 2 * p + q + 1)
                dve.tensor_tensor(v1[:, q, :, 0:D], psP[:, q, :].rearrange("p (t d) -> p t d", t=TILES),
                                  wide(vb_row[:, :]), ALU.add).then_inc(v_ready, 1)

            def p_elu(p, k):
                dve.wait_ge(k_exp if k else q_exp, p + 1)
                dve.scalar_tensor_tensor(out=(qT, kT)[k][:, :], in0=(eQ, eK)[k].rearrange("p t d -> p (t d)"), scalar=1.0,
                                         in1=(rQ, rK)[k], op0=ALU.min, op1=ALU.add).then_inc(kT_ready if k else qT_ready, 1)

            def a_mask(s, t):
                dve.wait_ge(sc_ps, TILES * s + t + 1)
                dve.tensor_tensor(scT[:, :, :], psR[:, :, 0:P], wide(causal[:, :], 2), ALU.mult).then_inc(sc_ready, 1)

            def a_x1(s, t):
                n = TILES * s + t + 1
                if t == 0:
                    dve.wait_ge(hb_ready, 2 * s + 2)
                dve.wait_ge(num_ps, n)
                dve.tensor_scalar(den[:, :], psR[:, :, NUM + D], ATTN_EPS, None, ALU.add).then_inc(den_ready, 1)
                dve.tensor_tensor(state[0:F, :], state[0:F, :], psR[0:F, 0, KV:KV + D + 1], ALU.add)
                dve.wait_ge(den_ready, n)
                dve.reciprocal(rden[:, :], den[:, :]).then_inc(rden_ready, 1)
                dve.tensor_tensor(state[F:P, :], state[F:P, :], psR[F:P, 1, KV:KV + D + 1], ALU.add).then_inc(state_sum, 1)
                dve.wait_ge(rden_ready, n)
                for q in range(2):
                    last = dve.scalar_tensor_tensor(out=x1[:, q, t, :], in0=psR[:, q, NUM:NUM + D], scalar=rden[:, q:q + 1],
                                                    in1=hb[:, q, t, :], op0=ALU.mult, op1=ALU.add)
                last.then_inc(x1_ready, 1)
                if t == TILES - 1:
                    dve.wait_ge(state_sum, n)
                    dve.tensor_scalar(state[:, :], state[:, :], carry[:, bass.ds(s, 1)], None, ALU.mult).then_inc(state_ready, 1)

            def a_x1stats(s, t):
                dve.wait_ge(x1_ready, TILES * s + t + 1)
                for q in range(2):
                    last = bn("x1", x1[:, q, t, :], q * TILES + t)
                if t == TILES - 1:
                    last.then_inc(st_done["x1"], 1)

            def a_norm2(s):
                dve.wait_ge(rstd_done["x1"], s + 1)
                for q in range(2):
                    normalise(un, x1, "x1", q).then_inc(u2_ready, 1)

            def a_u2lo(s, q):
                dve.wait_ge(u2hi, 2 * s + q + 1)
                dve.tensor_tensor(u2T_l[:, q, :], psR[:, q, :], u2T_h[:, q, :].bitcast(F32), ALU.subtract).then_inc(u2lo, 1)

            def a_ghi(s, i):
                dve.wait_ge(gelu_done, 2 * FC * s + i + 1)
                dve.tensor_copy(ghi[:, i % 3, :], gf[:, i % 2, :]).then_inc(g_hi, 1)

            def a_X(s, q):
                dve.wait_ge(y2T_ps, 2 * s + q + 1)
                dve.wait_ge(xg_ready, 2 * s + q + 1)
                if q == 0 and not (isinstance(s, int) and s == 0):
                    dve.wait_ge(Xo_ready, 16 * s)
                dve.tensor_tensor(X[:, q, :, :], psR[:, q, :].rearrange("p (t d) -> p t d", t=TILES), xg[:, q, :, :],
                                  ALU.add).then_inc(X_ready, 1)

            def a_stats3(s):
                for q in range(2):
                    dve.wait_ge(X_ready, 2 * s + q + 1)
                    for t in range(TILES):
                        last = bn("X", X[:, q, t, :], q * TILES + t)
                last.then_inc(st_done["X"], 1)
                aggregate("X", s)

            def a_norm3(s):
                dve.wait_ge(rstd_done["X"], s + 1)
                for q in range(2):
                    normalise(un, X, "X", q).then_inc(u3_ready, 1)

            def a_h2hi(s, q):
                dve.wait_ge(h2_ready, 2 * s + q + 1)
                dve.tensor_copy(h2_h[:, q, :], h2T[:, q, :]).then_inc(h2hi, 1)

            def a_route(s, part):
                done = [(0, 9)[part]]

                def then(ins):
                    done[0] += 1
                    ins.then_inc(route, 1)
                    stand_alone(dve, route, ROUTE * s + done[0])

                if part == 0:
                    dve.wait_ge(tanh_done, s + 1)
                    then(dve.tensor_scalar(score[:, :, :], th[:, :, :], 0.5, 0.5, ALU.mult, ALU.add))
                    then(dve.tensor_tensor(biased[:, :, :], score[:, :, :], wide(gb_row[:, :], 8), ALU.add))
                    then(dve.tensor_reduce(gmax[:, :], biased[:, :, :].rearrange("p k (g e) -> p (k g) e", g=NG), AX.X, ALU.max))
                    gm = gmax[:, :].rearrange("p (k g) -> p k g", g=NG)
                    other = gm.unsqueeze(2).to_broadcast([P, 8, NG, NG])
                    own = gm.unsqueeze(3).to_broadcast([P, 8, NG, NG])
                    then(dve.tensor_tensor(gt[:, :, :, :], other, own, ALU.is_gt))
                    then(dve.tensor_tensor(ge[:, :, :, :], other, own, ALU.is_ge))
                    low = lower[:, :].unsqueeze(1).to_broadcast([P, 8, NG * NG])
                    ge_f = ge[:, :, :, :].rearrange("p k g e -> p k (g e)")
                    gt_f = gt[:, :, :, :].rearrange("p k g e -> p k (g e)")
                    then(dve.tensor_tensor(ge_f, ge_f, low, ALU.mult))
                    then(dve.tensor_tensor(gt_f, gt_f, ge_f, ALU.max))
                    then(dve.tensor_reduce(rank[:, :], gt[:, :, :, :].rearrange("p k g e -> p (k g) e"), AX.X, ALU.add))
                    then(dve.tensor_scalar(penalty[:, :, :].rearrange("p k g -> p (k g)"), rank[:, :], 1.5, MASKED,
                                           ALU.is_ge, ALU.mult))
                    return
                pen = penalty[:, :, :].unsqueeze(3).to_broadcast([P, 8, NG, E // NG])
                then(dve.tensor_tensor(cand[:, :, 0:E].rearrange("p k (g e) -> p k g e", g=NG),
                                       biased[:, :, :].rearrange("p k (g e) -> p k g e", g=NG), pen, ALU.add))
                for k in range(8):
                    last = dve.max(top[:, k, :], cand[:, k, 0:E])
                then(last)
                then(dve.memset(top[:, :, 4:8], SENTINEL))
                for k in range(8):
                    last = dve.match_replace(marked[:, k, :], top[:, k, :], cand[:, k, :], CHOSEN)
                then(last)
                then(dve.scalar_tensor_tensor(out=comb[:, :, :], in0=marked[:, :, 0:E], scalar=CHOSEN / 2, in1=score[:, :, :],
                                              op0=ALU.is_ge, op1=ALU.mult))
                then(dve.tensor_copy(parts[:, :, 0:E], comb[:, :, :]))
                then(dve.tensor_tensor(rest[:, :, :], comb[:, :, :], parts[:, :, 0:E], ALU.subtract))
                then(dve.tensor_copy(parts[:, :, E:2 * E], rest[:, :, :]))
                dve.tensor_tensor(parts[:, :, 2 * E:3 * E], rest[:, :, :], parts[:, :, E:2 * E], ALU.subtract).then_inc(parts_ready, 1)

            def c_hidden(c, n):
                q, uu = n // ALLU, n % ALLU
                dve.wait_ge(silu_done, 2 * ALLU * c + n + 1)
                if uu == UNITS:
                    dve.tensor_tensor(hid[F:P, n % 3, :], psA[F:P, :], g[F:P, n % 2, :], ALU.mult).then_inc(hid_ready, 1)
                    return
                i = 2 * UNITS * c + UNITS * q + uu + 1
                dve.wait_ge(w3_ps, i)
                dve.tensor_tensor(gu[:, n % 2, :], psB[:, :], g[:, n % 2, :], ALU.mult).then_inc(gu_ready, 1)
                dve.wait_ge(gu_ready, i)
                dve.wait_ge(comb_ps, i)
                dve.tensor_tensor(hid[:, n % 3, :], psC[:, :], gu[:, n % 2, :], ALU.mult).then_inc(hid_ready, 1)

            def c_out(c, q):
                dve.wait_ge(yT_ps, 2 * c + q + 1)
                dve.wait_ge(Xo_ready, 16 * c + 16)
                if isinstance(c, int) and c > 0:
                    dve.wait_ge(stored[q], 16 * c)
                dve.tensor_tensor(o[:, q, :, :], psP[:, 1, :].rearrange("p (t d) -> p t d", t=TILES), Xo[:, q, :, :],
                                  ALU.add).then_inc(out_ready, 1)

            def split(hi, lo, src):
                chain(dve.tensor_copy(hi, src))
                return dve.tensor_tensor(lo, src, hi.bitcast(F32), ALU.subtract)

            def clamp_gate(v, tmp):
                chain(dve.tensor_scalar(tmp, v, 0.0, 2.0, ALU.is_ge, ALU.mult))
                chain(dve.tensor_scalar(tmp, tmp, 1.0, None, ALU.subtract))
                chain(dve.tensor_tensor(v, v, tmp, ALU.mult))
                return dve.scalar_tensor_tensor(out=v, in0=v, scalar=0.25, in1=tmp, op0=ALU.max, op1=ALU.mult)

            dve.memset(v1[:, :, :, D:D + 1], 1.0)
            dve.memset(cand[:, :, E:E + 4], SENTINEL)
            dve.memset(state[:, :], 0.0).then_inc(state_ready, 1)
            dve.wait_ge(s_silu, 1)
            dve.tensor_copy(flat(cspread).rearrange("p (b m) -> p b m", b=NSEQ),
                            silu_c[:, :].unsqueeze(2).to_broadcast([P, NSEQ, P])).then_inc(s_cb, 1)
            m_stats(0)
            for b in range(NSEQ):
                dve.wait_ge(s_modr_ps, b + 1)
                dve.tensor_copy(modr[:, :, b, :], banks[b][:, 0:3 * D].rearrange("p (r d) -> p r d", r=3)).then_inc(s_modr_cp, 1)
            dve.wait_ge(s_modr_cp, NSEQ)
            row = lambda r: modr[:, r, :, :].rearrange("p b d -> p (b d)")
            chain(dve.tensor_scalar(row(ROW_CA), row(ROW_CA), 1.0, None, ALU.add))
            clamp_gate(row(ROW_GA), flat(un)).then_inc(s_modr, 1)
            m_norm(0)
            dve.wait_ge(s_modc_ps, 1)
            chain(dve.tensor_copy(modc[:, :, :], psA[:, 0:4 * NSEQ].rearrange("p (j b) -> p j b", j=4)))
            chain(dve.tensor_scalar(modc[:, CB, :], modc[:, CB, :], 1.0, None, ALU.add))
            chain(clamp_gate(modc[:, GA, :], rank[:, 0:NSEQ]))
            chain(clamp_gate(modc[:, GB, :], rank[:, 0:NSEQ]))
            dve.wait_ge(small_in, 16 * len(SMALL))
            chain(dve.tensor_scalar(gaf2b[:, :], modc[:, GA, :], vecs[:, F2B:F2B + 1], None, ALU.mult))
            dve.wait_ge(s_fold_ps, 1)
            chain(dve.tensor_copy(wvo, psB[:, 0:D]))
            dve.tensor_copy(ln1b_sp, vecs[:, LN1B:LN1B + 1].to_broadcast([P, P]))
            dve.tensor_copy(vb_sp, vecs[:, VB:VB + 1].to_broadcast([P, P])).then_inc(s_wvo, 1)
            chain(dve.tensor_tensor(bq[:, :], psC[:, 0:2], vecs[:, QB:QB + 2], ALU.add))
            chain(dve.tensor_tensor(f1bias[:, :], psY[:, 0:FC], f1b[:, :], ALU.add))
            dve.wait_ge(attn_in, 16 * len(ATTN))
            qk = raw_qk[:, :]
            chain(dve.tensor_scalar(qk, qk, vecs[:, LN1W:LN1W + 1], None, ALU.mult))
            split(wqk_h[:, :, :].rearrange("p a b -> p (a b)"), wqk_l[:, :, :].rearrange("p a b -> p (a b)"), qk)
            dve.wait_ge(s_vb_ps, 1)
            chain(dve.tensor_copy(vb_row[:, :], psR[:, 0, 0:D]))
            chain(dve.tensor_scalar(wvo, wvo, vecs[:, LN1W:LN1W + 1], None, ALU.mult))
            split(wv_h[:, :], wv_l[:, :], wvo)
            chain(dve.tensor_scalar(raw_f1[:, 0, :], raw_f1[:, 0, :], vecs[:, LN2W:LN2W + 1], None, ALU.mult))
            split(f1_h[:, :, :].rearrange("p a b -> p (a b)"), f1_l[:, :, :].rearrange("p a b -> p (a b)"), raw_f1[:, 0, :]).then_inc(s_weights, 1)

            p_stats(0)
            p_norm(0)
            for q in range(2):
                p_u1lo(0, q)
            m_stats(1)
            for q in range(2):
                p_v(0, q)
            m_norm(1)
            for k in range(2):
                p_elu(0, k)
            dve.wait_ge(moe_in, 16 * len(MOE))
            for hi, lo, src in ((w1_h, w1_l, flat(raw_w1)), (w3_h, w3_l, flat(raw_w3)),
                                (w2_h, w2_l, raw_w2[:, :, :].rearrange("p a b -> p (a b)"))):
                split(hi[:, 0:UNITS, :].rearrange("p a b -> p (a b)"), lo[:, 0:UNITS, :].rearrange("p a b -> p (a b)"), src)
            split(w1_h[:, UNITS, :], w1_l[:, UNITS, :], raw_sh[:, 0, 0:P])
            split(w2_h[F:P, UNITS, :], w2_l[F:P, UNITS, :], raw_sh[F:P, 1, 0:P])
            split(f2_h[:, :, :].rearrange("p a b -> p (a b)"), f2_l[:, :, :].rearrange("p a b -> p (a b)"), raw_f2[:, 0, :]).then_inc(s_weights, 1)

            def iteration(c, s, p, m):
                if p is not None:
                    p_stats(p)
                for n in range(2 * ALLU + 2):
                    if n == ALLU and s is not None:
                        for i in range(2 * FC):
                            a_ghi(s, i)
                        a_X(s, 0)
                        a_X(s, 1)
                        if p is not None:
                            p_elu(p, 0)
                            p_elu(p, 1)
                    if s is not None and n < TILES:
                        a_mask(s, n)
                    if c is not None and n < 2 * ALLU:
                        c_hidden(c, n)
                    if s is not None and n < TILES:
                        a_x1(s, n)
                        a_x1stats(s, n)
                        if n == TILES - 1:
                            aggregate("x1", s)
                    if p is not None and n == 2:
                        p_norm(p)
                    if p is not None and n == 5:
                        p_u1lo(p, 0)
                        p_u1lo(p, 1)
                    if s is not None and n == 5:
                        a_norm2(s)
                    if p is not None and n == 6:
                        p_v(p, 0)
                        p_v(p, 1)
                    if s is not None and n == 8:
                        a_u2lo(s, 0)
                        a_u2lo(s, 1)
                    if m is not None and n == 10:
                        m_stats(m)
                    if s is not None and n == 11:
                        a_stats3(s)
                    if c is not None and n == 12:
                        c_out(c, 0)
                    if m is not None and n == 12:
                        m_norm(m)
                    if s is not None and n == 13:
                        a_norm3(s)
                    if s is not None and n == 15:
                        a_h2hi(s, 0)
                    if s is not None and n == 16:
                        a_route(s, 0)
                    if s is not None and n == 17:
                        a_route(s, 1)
                    if s is not None and n == 18:
                        a_h2hi(s, 1)
                if c is not None:
                    c_out(c, 1)

            iterations(dve, iteration)


def kernel(**inputs):
    import ml_dtypes
    import numpy as np

    import concourse.bacc as bacc
    from concourse.bass_utils import run_bass_kernel_spmd

    def get(name):
        return np.asarray(inputs["L0_" + name])

    qT, kT = get("attn_q_w").T, get("attn_k_w").T
    none = np.zeros_like(qT)
    two = lambda v: np.concatenate([v, v])
    vecs = [get("attn_ln1_w"), get("attn_ln1_b"), get("attn_ln2_w"), get("attn_ln2_b"), two(get("attn_q_b")),
            two(get("attn_k_b")), get("attn_v_b"), get("attn_f2_b")]
    chunks = lambda wT: wT.reshape(-1, P, wT.shape[1]).transpose(1, 0, 2).reshape(P, -1)
    w2 = get("ffn_w2").transpose(0, 2, 1).reshape(E * F, D)
    index = np.arange(P)
    group = np.arange(NG)
    spread = np.arange(3 * E)[:, None, None] % E == 2 * np.arange(UNITS)[:, None] + index // F
    arrays = {
        "x": get("attn_x").reshape(-1, D),
        "cT": get("c").T, "wmod": get("wmod"), "vecs": np.stack(vecs, axis=1),
        "f1b": get("attn_f1_b").reshape(FC, P).T,
        "v_w": get("attn_v_w"), "o_wT": get("attn_o_w").T,
        "qk_wT": np.concatenate([qT, none, none, qT, kT, none, none, kT], axis=1),
        "f1_wT": get("attn_f1_w").T, "f2_wT": chunks(get("attn_f2_w").T),
        "o_b": get("attn_o_b"), "gate_b": get("ffn_gate_bias"), "gate_wT": get("ffn_gate_w").T,
        "w1T": get("ffn_w1").reshape(E * F, D).T, "w3T": get("ffn_w3").reshape(E * F, D).T,
        "w2T": chunks(w2),
        "ws13T": np.concatenate([get("ffn_ws1").T, get("ffn_ws3").T], axis=1), "ws2T": get("ffn_ws2").T,
        "ident": np.eye(P, dtype=np.float32), "ident_b": np.eye(P, dtype=ml_dtypes.bfloat16),
        "causal": (index[:, None] <= index).astype(np.float32),
        "lower": np.tile((group < group[:, None]).astype(np.float32).reshape(1, -1), (P, 1)),
        "carry": np.tile((np.arange(STEPS) % 2 == 0).astype(np.float32), (P, 1)),
        "sel": spread.astype(ml_dtypes.bfloat16).reshape(3 * E, -1),
    }
    arrays = {n: np.ascontiguousarray(v) for n, v in arrays.items()}

    nc = bacc.Bacc("TRN2", target_bir_lowering=False, num_devices=1)
    a = {n: nc.dram_tensor(f"in_{n}", v.shape, mybir.dt.from_np(v.dtype), kind="ExternalInput").ap()
         for n, v in arrays.items()}
    a["o_b_row"] = a["o_b"].partition_broadcast(P)
    a["gate_b_row"] = a["gate_b"].partition_broadcast(P)
    a["out"] = nc.dram_tensor("out", arrays["x"].shape, F32, kind="ExternalOutput").ap()
    layer_kernel(nc, a)
    r = run_bass_kernel_spmd(nc, [{f"in_{n}": v for n, v in arrays.items()}], core_ids=[0])
    return r.results[0]["out"].reshape(inputs["L0_attn_x"].shape)
```

```python
from contextlib import ExitStack

import concourse.bass as bass
from concourse import mybir

F32 = mybir.dt.float32
F32R = mybir.dt.float32r
BF16 = mybir.dt.bfloat16
ALU = mybir.AluOpType
ACT = mybir.ActivationFunctionType
AX = mybir.AxisListType

P = 128
D = 128
F = 64
NSEQ = 8
STEPS = 8
TILES = 4
W = TILES * P
E = 16
NG = 4
UNITS = 8
ALLU = UNITS + 1
FC = 4
LN_EPS = 1e-5
ATTN_EPS = 1e-6
MASKED = -1e30
SENTINEL = -2e30
CHOSEN = 2e30
MLP_SLOT = 6
GA, SB, CB, GB = range(4)
ROW_SA, ROW_CA, ROW_GA = range(3)


def layer_kernel(nc, a):
    x_v = a["x"].rearrange("(q s t p) d -> q s p t d", q=2, s=STEPS, t=TILES)
    out_v = a["out"].rearrange("(q s t p) d -> q s p t d", q=2, s=STEPS, t=TILES)

    with ExitStack() as ctx:
        def sb(name, shape, dt=F32):
            return ctx.enter_context(nc.sbuf_tensor(name, shape, dt))

        def ps(name, shape):
            return ctx.enter_context(nc.psum_tensor(name, shape, F32))

        def sem(name):
            return ctx.enter_context(nc.semaphore(name))

        ident = sb("ident", [P, P])
        ident_b = sb("ident_b", [P, P], BF16)
        causal = sb("causal", [P, P])
        lower = sb("lower", [P, NG * NG])
        sel = sb("sel", [3 * E, UNITS, P], BF16)
        carry = sb("carry", [P, STEPS])
        vecs = sb("vecs", [P, 8])
        f1b = sb("f1b", [P, FC])
        cT = sb("cT", [P, NSEQ])
        silu_c = sb("silu_c", [P, NSEQ])
        ob_row = sb("ob_row", [P, D])
        gb_row = sb("gb_row", [P, E])
        expo = sb("expo", [P, 2 * TILES])
        minus = sb("minus", [P, 2 * TILES])
        eps = sb("eps", [P, 2 * TILES])
        gate_w = sb("gate_w", [P, E])
        modr = sb("modr", [P, 3, NSEQ, D])
        modc = sb("modc", [P, 4, NSEQ])
        gaf2b = sb("gaf2b", [P, NSEQ])
        bq = sb("bq", [P, 2])
        vb_row = sb("vb_row", [P, D])
        f1bias = sb("f1bias", [P, FC])
        wqk_h = sb("wqk_h", [P, 4, P], F32R)
        wqk_l = sb("wqk_l", [P, 4, P], F32R)
        wv_h = sb("wv_h", [P, D], F32R)
        wv_l = sb("wv_l", [P, D], F32R)
        f1_h = sb("f1_h", [P, FC, P], F32R)
        f1_l = sb("f1_l", [P, FC, P], F32R)
        f2_h = sb("f2_h", [P, FC, P], F32R)
        f2_l = sb("f2_l", [P, FC, P], F32R)
        w1_h = sb("w1_h", [P, ALLU, P], F32R)
        w1_l = sb("w1_l", [P, ALLU, P], F32R)
        w3_h = sb("w3_h", [P, UNITS, P], F32R)
        w3_l = sb("w3_l", [P, UNITS, P], F32R)
        w2_h = sb("w2_h", [P, ALLU, P], F32R)
        w2_l = sb("w2_l", [P, ALLU, P], F32R)

        xa = sb("xa", [P, 2, TILES, D])
        xb = sb("xb", [P, 2, TILES, D])
        u = sb("u", [P, 2, TILES, D])
        h = sb("h", [P, 2, TILES, D])
        hb = sb("hb", [P, 2, TILES, D])
        u1 = sb("u1", [P, 2, TILES, D])
        u1T_h = sb("u1T_h", [P, 2, W], F32R)
        u1T_l = sb("u1T_l", [P, 2, W], F32R)
        qT = sb("qT", [P, W])
        kT = sb("kT", [P, W])
        kt = sb("kt", [P, TILES, P])
        v1 = sb("v1", [P, 2, TILES, D + 1])
        scT = sb("scT", [P, 2, 2, P])
        den = sb("den", [P, 2, 2])
        rden = sb("rden", [P, 2, 2])
        state = sb("state", [P, D + 1])
        x1 = sb("x1", [P, 2, TILES, D])
        un = sb("un", [P, 2, TILES, D])
        u2T_h = sb("u2T_h", [P, 2, W], F32R)
        u2T_l = sb("u2T_l", [P, 2, W], F32R)
        gf = sb("gf", [P, 2, W])
        ghi = sb("ghi", [P, 3, W], F32R)
        glo = sb("glo", [P, 3, W], F32R)
        y2 = sb("y2", [P, 2, W])
        xg = sb("xg", [P, 2, TILES, D])
        X = sb("X", [P, 2, TILES, D])
        Xo = sb("Xo", [P, 2, TILES, D])
        h2T = sb("h2T", [P, 2, W])
        h2_h = sb("h2_h", [P, 2, W], F32R)
        h2_l = sb("h2_l", [P, 2, W], F32R)
        combT = sb("combT", [3 * E, 2 * W], BF16)
        stats = {n: sb(f"st_{n}", [P, 8, 6]) for n in ("x", "h", "x1", "X")}
        mv = {n: sb(f"mv_{n}", [P, 8, 2]) for n in stats}
        ve = {n: sb(f"ve_{n}", [P, 8]) for n in stats}
        rstd = {n: sb(f"rstd_{n}", [P, 8]) for n in stats}
        negm = {n: sb(f"negm_{n}", [P, 8]) for n in stats}
        shift = {n: sb(f"shift_{n}", [P, 8]) for n in stats}
        th = sb("th", [P, 8, E])
        score = sb("score", [P, 8, E])
        biased = sb("biased", [P, 8, E])
        gmax = sb("gmax", [P, 8 * NG])
        gt = sb("gt", [P, 8, NG, NG])
        ge = sb("ge", [P, 8, NG, NG])
        rank = sb("rank", [P, 8 * NG])
        penalty = sb("penalty", [P, 8, NG])
        cand = sb("cand", [P, 8, E + 4])
        top = sb("top", [P, 8, 8])
        marked = sb("marked", [P, 8, E + 4])
        comb = sb("comb", [P, 8, E])
        rest = sb("rest", [P, 8, E])
        parts = sb("parts", [P, 8, 3 * E], BF16)
        g = sb("g", [P, 2, W])
        gu = sb("gu", [P, 2, W])
        hid = sb("hid", [P, 3, W])
        hid_h = sb("hid_h", [P, 3, W], F32R)
        hid_l = sb("hid_l", [P, 3, W], F32R)
        y = sb("y", [P, W])
        o = sb("o", [P, 2, TILES, D])
        eQ, eK = u1[:, 0, :, :], u1[:, 1, :, :]

        psA, psB, psC, psY = ps("psA", [P, W]), ps("psB", [P, W]), ps("psC", [P, W]), ps("psY", [P, W])
        psR = ps("psR", [P, 2, W])
        psP = ps("psP", [P, 2, W])
        banks = [psA[:, :], psB[:, :], psC[:, :], psY[:, :], psR[:, 0, :], psR[:, 1, :], psP[:, 0, :], psP[:, 1, :]]
        GLO_POOL = (5,)

        def wait_glo(eng, s, i):
            mine = [k for k in range(2 * FC) if (k in GLO_POOL) == (i in GLO_POOL)]
            eng.wait_ge(g_lo_pool if i in GLO_POOL else g_lo_dve, len(mine) * s + mine.index(i) + 1)

        def yT_of(q):
            return psY[:, :] if q else psP[:, 1, :]

        scores, nums, kv = psP[:, :, 0:P], psR[:, :, 0:D + 1], psR[:, 0, D + 4:2 * D + 5]

        small_in, attn_in, moe_in = sem("small_in"), sem("attn_in"), sem("moe_in")
        s_silu, s_cb, s_modr_ps, s_modr_cp, s_modc_ps, s_setup = (
            sem(n) for n in ("c_silu", "c_spread", "modr_ps", "modr_copied", "modc_ps", "setup_step"))
        s_fold_ps, s_wvo, s_vb_ps, s_modr, s_weights, s_pool0 = (
            sem(n) for n in ("fold_ps", "wvo_ready", "vbias_ps", "modr_ready", "weights_ready", "pool_consts"))
        xa_in = [sem("xa_in0"), sem("xa_in1")]
        xb_in = [sem("xb_in0"), sem("xb_in1")]
        stored = [sem("stored0"), sem("stored1")]
        st_done = {n: sem(f"stats_{n}") for n in stats}
        mv_done = {n: sem(f"mean_var_{n}") for n in stats}
        ve_done = {n: sem(f"var_eps_{n}") for n in stats}
        rstd_done = {n: sem(f"rstd_{n}") for n in stats}
        negm_done = {n: sem(f"neg_mean_{n}") for n in shift}
        shift_done = {n: sem(f"shift_{n}") for n in shift}
        names = """u_ready u_scaled h_ready hb_ready u1_ready u1T_ps u1hi u1lo q_ps k_ps q_relu k_relu qT_ready
            kT_ready v_ps v_ready kt_ps kt_ready sc_ps sc_ready num_ps den_ready rden_ready x1_ready state_sum
            state_ready u2_ready u2b_ready u2T_ps u2hi u2hi_dve u2lo x1_gated xg_ready f1_ps gelu_done g_hi g_lo_dve g_lo_pool f2_ps y2_ready
            y2T_ps X_ready Xo_ready u3_ready u3b_ready u3T_ps h2_ready h2hi h2lo gate_ps tanh_done route parts_ready
            parts_ps combT_ready w1_ps w3_ps comb_ps silu_done gu_ready hid_ready hid_hi hid_lo w2_ps y_ready
            yT_ps out_ready""".split()
        S = {n: sem(n) for n in names}
        (u_ready, u_scaled, h_ready, hb_ready, u1_ready, u1T_ps, u1hi, u1lo, q_ps, k_ps, q_relu, k_relu, qT_ready,
         kT_ready, v_ps, v_ready, kt_ps, kt_ready, sc_ps, sc_ready, num_ps, den_ready, rden_ready, x1_ready, state_sum,
         state_ready, u2_ready, u2b_ready, u2T_ps, u2hi, u2hi_dve, u2lo, x1_gated, xg_ready, f1_ps, gelu_done, g_hi, g_lo_dve, g_lo_pool, f2_ps, y2_ready,
         y2T_ps, X_ready, Xo_ready, u3_ready, u3b_ready, u3T_ps, h2_ready, h2hi, h2lo, gate_ps, tanh_done, route, parts_ready,
         parts_ps, combT_ready, w1_ps, w3_ps, comb_ps, silu_done, gu_ready, hid_ready, hid_hi, hid_lo, w2_ps, y_ready,
         yT_ps, out_ready) = (S[n] for n in names)

        ROUTE = 13

        def iterations(eng, iteration):
            iteration(None, 0, 1, 2)
            with eng.Fori(1, STEPS - 2) as t:
                iteration(t - 1, t, t + 1, t + 2)
            iteration(STEPS - 3, STEPS - 2, STEPS - 1, None)
            iteration(STEPS - 2, STEPS - 1, None, None)
            iteration(STEPS - 1, None, None, None)

        wait_value = {e.engine: e.alloc_register("wait_value") for e in (nc.sync, nc.tensor, nc.vector)}

        def stand_alone(eng, semaphore, value):
            if not isinstance(value, int):
                eng.reg_mov(wait_value[eng.engine], value)
                value = wait_value[eng.engine]
            eng.wait_ge(small_in, 16 * len(SMALL))
            eng.wait_ge(semaphore, value)

        row_order = sorted(range(NSEQ), key=lambda b: b % (NSEQ // 2))

        def seq(s, q):
            return s // 2 + NSEQ // 2 * q

        def wide(row, n=TILES):
            return row.unsqueeze(1).to_broadcast([P, n, row.shape[-1]])

        raw_w1, raw_w3, raw_w2 = X, Xo, h2T
        raw_f1, raw_f2 = g, gu
        raw_sh = hid
        raw_qk = y
        raw_v = o
        wmod = xg
        raw_vw, raw_owT = o[:, 0, 0, :], o[:, 0, 1, :]
        wvo = o[:, 0, 2, :]
        ln1b_sp, vb_sp = o[:, 1, 0, :], o[:, 1, 1, :]
        LN1W, LN1B, LN2W, LN2B, QB, KB, VB, F2B = range(8)
        cspread = x1
        flat = lambda t3: t3[:, :, :, :].rearrange("p a b c -> p (a b c)")

        SMALL = [(cT[:, :], "cT"), (flat(wmod)[:, 0:6 * D], "wmod"), (vecs[:, :], "vecs"), (f1b[:, :], "f1b")]
        ATTN = [(raw_vw, "v_w"), (raw_owT, "o_wT"), (raw_qk[:, :], "qk_wT"), (ident[:, :], "ident"),
                (causal[:, :], "causal"), (carry[:, :], "carry"), (raw_f1[:, 0, :], "f1_wT"),
                (ob_row[:, :], "o_b_row"), (gb_row[:, :], "gate_b_row")]
        MOE = [(flat(raw_w1), "w1T"), (flat(raw_w3), "w3T"), (raw_w2[:, :, :].rearrange("p a b -> p (a b)"), "w2T"),
               (raw_sh[:, 0, 0:P], "ws13T"), (raw_sh[F:P, 1, 0:P], "ws2T"), (raw_f2[:, 0, :], "f2_wT"),
               (gate_w[:, :], "gate_wT"), (ident_b[:, :], "ident_b"), (lower[:, :], "lower"),
               (sel[:, :, :].rearrange("k u m -> k (u m)"), "sel")]

        block = ctx.enter_context(nc.Block())

        @block.sync
        def _(sp):
            def rows_of(view, q, s):
                return view[q, bass.ds(s, 1), :, :, :].rearrange("o p t d -> (o p) t d")

            def load_x(dst, loaded, s):
                for q in range(2):
                    sp.dma_start(dst[:, q, :, :], rows_of(x_v, q, s)).then_inc(loaded[q], 16)

            def get(places, done):
                for dst, name in places:
                    sp.dma_start(dst, a[name]).then_inc(done, 16)

            get(SMALL, small_in)
            load_x(xa, xa_in, 0)
            get(ATTN, attn_in)
            get(MOE, moe_in)
            sp.wait_ge(u_ready, 2)
            load_x(xa, xa_in, 1)

            def iteration(c, s, p, m):
                if m is not None:
                    stand_alone(sp, u_ready, 2 * m)
                    load_x(xa, xa_in, m)
                if s is not None:
                    if not (isinstance(s, int) and s == 0):
                        stand_alone(sp, xg_ready, 2 * s)
                    load_x(xb, xb_in, s)
                if c is not None:
                    for q in range(2):
                        stand_alone(sp, out_ready, 2 * c + q + 1)
                        sp.dma_start(rows_of(out_v, q, c), o[:, q, :, :]).then_inc(stored[q], 16)
                if s is not None:
                    sp.wait_ge(X_ready, 2 * s + 2)
                    sp.dma_start(Xo[:, :, :, :], X[:, :, :, :]).then_inc(Xo_ready, 16)
                if c is not None:
                    for q in range(2):
                        stand_alone(sp, stored[q], 16 * c + 16)

            iterations(sp, iteration)

        @block.tensor
        def _(pe):
            def product(out, w_h, w_l, x_h, x_l, start=True, stop=True):
                pe.matmul(out, w_h, x_h, start=start, stop=False)
                pe.matmul(out, w_l, x_h, start=False, stop=False)
                return pe.matmul(out, w_h, x_l, start=False, stop=stop)

            pe.wait_ge(small_in, 16 * len(SMALL))
            pe.wait_ge(s_cb, 1)
            wm = flat(wmod)
            for b in row_order:
                pe.matmul(banks[b][:, 0:3 * D], cspread[:, b // TILES, b % TILES, :], wm[:, 0:3 * D],
                          start=True, stop=True).then_inc(s_modr_ps, 1)
            pe.wait_ge(s_modr_cp, NSEQ)
            for j in range(4):
                last = pe.matmul(psA[:, j * NSEQ:(j + 1) * NSEQ], wm[:, (2 + j) * D:(3 + j) * D], silu_c[:, :],
                                 start=True, stop=True)
            last.then_inc(s_modc_ps, 1)
            pe.wait_ge(attn_in, 16 * len(ATTN))
            pe.matmul(psB[:, 0:D], raw_vw, raw_owT, start=True, stop=True)
            for k in range(2):
                for q in range(2):
                    pe.matmul(psC[:, k:k + 1], raw_qk[:, (2 * k + q) * P:(2 * k + q + 1) * P], vecs[:, LN1B:LN1B + 1],
                              start=(q == 0), stop=(q == 1))
            for c in range(FC):
                last = pe.matmul(psY[:, c:c + 1], raw_f1[:, 0, c * P:(c + 1) * P], vecs[:, LN2B:LN2B + 1],
                                 start=True, stop=True)
            last.then_inc(s_fold_ps, 1)
            pe.wait_ge(s_wvo, 1)
            pe.matmul(psR[:, 0, 0:D], ln1b_sp, wvo, start=True, stop=False)
            pe.matmul(psR[:, 0, 0:D], vb_sp, raw_owT, start=False, stop=True).then_inc(s_vb_ps, 1)

            def transposes(bank, src, done):
                for t in range(TILES):
                    last = pe.transpose(bank[:, t * P:(t + 1) * P], src[:, t, :], ident[:, :])
                last.then_inc(done, 1)

            def p_transpose(p, q):
                pe.wait_ge(u1_ready, 2 * p + q + 1)
                if q == 0 and not (isinstance(p, int) and p == 0):
                    pe.wait_ge(sc_ready, TILES * p)
                transposes(psP[:, q, :], u1[:, q, :, :], u1T_ps)

            def p_v(p, q):
                pe.wait_ge(u1hi, 2 * p + q + 1)
                pe.wait_ge(u1lo, 2 * p + q + 1)
                for t in range(TILES):
                    cols = slice(t * P, (t + 1) * P)
                    last = product(psP[:, q, cols], u1T_h[:, q, cols], u1T_l[:, q, cols], wv_h[:, :], wv_l[:, :])
                last.then_inc(v_ps, 1)

            def p_qk(p, k):
                pe.wait_ge(v_ready, 2 * p + k + 1)
                for q in range(2):
                    last = product(psP[:, k, :], wqk_h[:, 2 * k + q, :], wqk_l[:, 2 * k + q, :],
                                   u1T_h[:, q, :], u1T_l[:, q, :], start=(q == 0), stop=(q == 1))
                last.then_inc(k_ps if k else q_ps, 1)

            def p_kt(p):
                pe.wait_ge(q_relu, p + 1)
                pe.wait_ge(kT_ready, p + 1)
                for t in range(TILES):
                    last = pe.transpose(psP[:, 0, t * P:(t + 1) * P], kT[:, t * P:(t + 1) * P], ident[:, :])
                last.then_inc(kt_ps, 1)

            def a_scores(c, s, t):
                if t == 0:
                    pe.wait_ge(qT_ready, s + 1)
                    pe.wait_ge(kT_ready, s + 1)
                    pe.wait_ge(kt_ready, s + 1)
                    pe.wait_ge(k_relu, s + 1)
                    if c is not None:
                        pe.wait_ge(out_ready, 2 * c + 1)
                else:
                    pe.wait_ge(sc_ready, TILES * s + t)
                cols = slice(t * P, (t + 1) * P)
                for q in range(2):
                    rows = slice(F * q, F * q + F)
                    last = pe.matmul(scores[:, q, :], kT[rows, cols], qT[rows, cols], start=True, stop=True)
                last.then_inc(sc_ps, 1)

            def a_sums(s, t):
                if t == 0:
                    pe.wait_ge(v_ready, 2 * s + 2)
                    pe.wait_ge(state_ready, s + 1)
                    if not (isinstance(s, int) and s == 0):
                        pe.wait_ge(tanh_done, s)
                        pe.wait_ge(combT_ready, s)
                else:
                    pe.wait_ge(x1_ready, TILES * s + t)
                for q in range(2):
                    rows = slice(F * q, F * q + F)
                    pe.matmul(kv[rows, :], kt[:, t, rows], v1[:, q, t, :], start=True, stop=True)
                pe.wait_ge(sc_ready, TILES * s + t + 1)
                if t:
                    pe.wait_ge(state_sum, TILES * s + t)
                cols = slice(t * P, (t + 1) * P)
                for q in range(2):
                    rows = slice(F * q, F * q + F)
                    pe.matmul(nums[:, q, :], scT[:, t % 2, q, :], v1[:, q, t, :], start=True, stop=False)
                    last = pe.matmul(nums[:, q, :], qT[rows, cols], state[rows, :], start=False, stop=True)
                last.then_inc(num_ps, 1)

            def a_transpose2(s, q):
                pe.wait_ge(u2b_ready if q else u2_ready, s + 1)
                transposes(psR[:, q, :], un[:, q, :, :], u2T_ps)

            def a_f1(c, s, i):
                q, j = i // FC, i % FC
                if j == 0:
                    pe.wait_ge(u2hi_dve if q else u2hi, s + 1)
                    pe.wait_ge(u2lo, 2 * s + q + 1)
                if c is not None and i == 0:
                    pe.wait_ge(silu_done, 2 * ALLU * c + MLP_SLOT)
                if c is not None and i == 1:
                    pe.wait_ge(gu_ready, 2 * UNITS * c + MLP_SLOT)
                if i >= 2:
                    pe.wait_ge(gelu_done, 2 * FC * s + i - 1)
                product((psA, psB)[i % 2][:, :], f1_h[:, j, :], f1_l[:, j, :], u2T_h[:, q, :],
                        u2T_l[:, q, :]).then_inc(f1_ps, 1)

            def a_f2(s, i):
                q, j = i // FC, i % FC
                pe.wait_ge(g_hi, 2 * FC * s + i + 1)
                wait_glo(pe, s, i)
                product(psR[:, q, :], f2_h[:, j, :], f2_l[:, j, :], ghi[:, i % 3, :], glo[:, i % 3, :],
                        start=(j == 0), stop=(j == FC - 1)).then_inc(f2_ps, 1)

            def a_y2T(s, q):
                pe.wait_ge(y2_ready, 2 * s + q + 1)
                for t in range(TILES):
                    last = pe.transpose(psR[:, q, t * P:(t + 1) * P], y2[:, q, t * P:(t + 1) * P], ident[:, :])
                last.then_inc(y2T_ps, 1)

            def a_transpose3(s, q):
                pe.wait_ge(u3b_ready if q else u3_ready, s + 1)
                transposes(psR[:, q, :], un[:, q, :, :], u3T_ps)

            def a_gate(s):
                pe.wait_ge(h2_ready, 2 * s + 2)
                for k in range(8):
                    last = pe.matmul(psR[:, 0, k * E:(k + 1) * E], h2T[:, k // TILES, (k % TILES) * P:(k % TILES + 1) * P],
                                     gate_w[:, :], start=True, stop=True)
                last.then_inc(gate_ps, 1)

            def a_parts(s):
                stand_alone(pe, parts_ready, s + 1)
                wb = psR[:, 1, :].bitcast(BF16)
                for k in range(8):
                    last = pe.transpose(wb[0:3 * E, k * P:(k + 1) * P], parts[:, k, :], ident_b[:, :])
                last.then_inc(parts_ps, 1)

            def c_up(c, n, s):
                q, uu = n // ALLU, n % ALLU
                if uu == 0:
                    pe.wait_ge(h2hi, 2 * c + q + 1)
                    pe.wait_ge(h2lo, 2 * c + q + 1)
                if uu == UNITS:
                    pe.wait_ge(hid_ready, 2 * ALLU * c + n)
                    product(psC[:, :], w1_h[:, uu, :], w1_l[:, uu, :], h2_h[:, q, :], h2_l[:, q, :]).then_inc(w1_ps, 1)
                    return
                first = isinstance(c, int) and c == 0 and n == 0
                if first:
                    pe.wait_ge(gelu_done, 2 * FC)
                else:
                    pe.wait_ge(silu_done, 2 * ALLU * c + n - (uu == 0))
                if n == MLP_SLOT and s is not None:
                    pe.wait_ge(gelu_done, 2 * FC * s + 2 * FC - 1)
                product(psA[:, :], w1_h[:, uu, :], w1_l[:, uu, :], h2_h[:, q, :], h2_l[:, q, :]).then_inc(w1_ps, 1)
                if not first:
                    pe.wait_ge(gu_ready, 2 * UNITS * c + UNITS * q + uu)
                if n == MLP_SLOT and s is not None:
                    pe.wait_ge(gelu_done, 2 * FC * s + 2 * FC)
                product(psB[:, :], w3_h[:, uu, :], w3_l[:, uu, :], h2_h[:, q, :], h2_l[:, q, :]).then_inc(w3_ps, 1)

            def c_comb(c, n):
                q, uu = n // ALLU, n % ALLU
                if uu == UNITS:
                    return
                if n == 0:
                    pe.wait_ge(combT_ready, c + 1)
                if n:
                    pe.wait_ge(hid_ready, 2 * ALLU * c + n)
                pe.matmul(psC[:, :], sel[:, uu, :], combT[:, q * W:(q + 1) * W], start=True, stop=True).then_inc(comb_ps, 1)

            def c_down(c, n, s):
                q, uu = n // ALLU, n % ALLU
                pe.wait_ge(hid_hi, 2 * ALLU * c + n + 1)
                pe.wait_ge(hid_lo, 2 * ALLU * c + n + 1)
                if n == ALLU:
                    pe.wait_ge(y_ready, 2 * c + 1)
                if n == 0 and s is None:
                    pe.wait_ge(out_ready, 2 * c)
                rows = slice(0, P) if uu < UNITS else slice(F, P)
                product(psY[:, :], w2_h[rows, uu, :], w2_l[rows, uu, :], hid_h[rows, n % 3, :], hid_l[rows, n % 3, :],
                        start=(uu == 0), stop=(uu == UNITS)).then_inc(w2_ps, 1)

            def c_yT(c, q):
                pe.wait_ge(y_ready, 2 * c + q + 1)
                if q == 0:
                    pe.wait_ge(k_relu, min(c + 3, STEPS) if isinstance(c, int) else c + 3)
                for t in range(TILES):
                    last = pe.transpose(yT_of(q)[:, t * P:(t + 1) * P], y[:, t * P:(t + 1) * P], ident[:, :])
                last.then_inc(yT_ps, 1)

            for q in range(2):
                p_transpose(0, q)
            pe.wait_ge(s_weights, 1)
            for q in range(2):
                p_v(0, q)
            for k in range(2):
                p_qk(0, k)
            p_kt(0)
            a_scores(None, 0, 0)
            a_scores(None, 0, 1)
            a_sums(0, 0)

            def iteration(c, s, p, m):
                for n in range(2 * ALLU + 2):
                    mlp = n == MLP_SLOT and s is not None
                    shared = n % ALLU == UNITS
                    if mlp:
                        if c is None:
                            pe.wait_ge(s_weights, 2)
                            pe.wait_ge(moe_in, 16 * len(MOE))
                        for i in range(2 * FC + 2):
                            if i < 2 * FC:
                                a_f1(c, s, i)
                            if c is not None and i == 1:
                                c_down(c, n - 2, s)
                            if c is not None and i == 2 * FC:
                                c_up(c, n, s)
                                c_comb(c, n)
                            if i >= 2:
                                a_f2(s, i - 2)
                    if s is not None and n == 18:
                        c_up(s, 0, None)
                    if p is not None and n == (17 if c is not None else 9):
                        p_kt(p)
                    if c is not None and shared:
                        c_down(c, n - 2, s)
                    if c is not None and 1 <= n < 2 * ALLU and not mlp:
                        c_up(c, n, s)
                    if s is not None and 1 <= n < TILES - 1:
                        a_scores(None, s, n + 1)
                    if p is not None and n == 3:
                        p_transpose(p, 0)
                        p_transpose(p, 1)
                    if s is not None and n == 7:
                        a_y2T(s, 0)
                        a_y2T(s, 1)
                    if c is not None and 1 <= n < 2 * ALLU and not mlp:
                        c_comb(c, n)
                    if s is not None and n == 11:
                        a_transpose3(s, 0)
                        a_transpose3(s, 1)
                    if s is not None and n == 12:
                        a_gate(s)
                    if p is not None and n == 5:
                        p_qk(p, 0)
                    if s is not None and n == 5:
                        a_transpose2(s, 0)
                        a_transpose2(s, 1)
                    if p is not None and n == 5:
                        p_qk(p, 1)
                    if p is not None and n == (2 * ALLU + 1 if c is not None else 13):
                        a_scores(None, p, 1)
                    if c is not None and n >= 2 and not shared and not mlp:
                        c_down(c, n - 2, s)
                    if s is not None and 1 <= n < TILES:
                        a_sums(s, n)
                    if p is not None and n == 4:
                        p_v(p, 0)
                        p_v(p, 1)
                    if c is not None and n == 12:
                        c_yT(c, 0)
                    if p is not None and n == (18 if c is not None else 11):
                        a_scores(c, p, 0)
                    if s is not None and n == 18:
                        a_parts(s)
                if s is not None:
                    c_comb(s, 0)
                if p is not None:
                    a_sums(p, 0)
                if c is not None:
                    c_yT(c, 1)

            iterations(pe, iteration)

        @block.scalar
        def _(act):
            act.wait_ge(small_in, 16 * len(SMALL))
            act.activation(silu_c[:, :], cT[:, :], ACT.Silu).then_inc(s_silu, 1)

            def normalise(dst, src, name, q):
                for t in range(TILES):
                    k = q * TILES + t
                    last = act.activation(dst[:, q, t, :], src[:, q, t, :], ACT.Identity, scale=rstd[name][:, k:k + 1],
                                          bias=shift[name][:, k:k + 1])
                return last

            def m_norm(m, q):
                act.wait_ge(shift_done["x"], m + 1)
                normalise(u, xa, "x", q).then_inc(u_ready, 1)

            def p_norm(p, q):
                act.wait_ge(shift_done["h"], p + 1)
                if not (isinstance(p, int) and p == 0):
                    act.wait_ge(kT_ready, p)
                normalise(u1, h, "h", q).then_inc(u1_ready, 1)

            def p_u1hi(p, q):
                act.wait_ge(u1T_ps, 2 * p + q + 1)
                act.activation(u1T_h[:, q, :], psP[:, q, :], ACT.Copy).then_inc(u1hi, 1)

            def p_exp(p, k):
                act.wait_ge(k_ps if k else q_ps, p + 1)
                act.activation((eQ, eK)[k].rearrange("p t d -> p (t d)"), psP[:, k, :], ACT.Exp, bias=bq[:, k:k + 1])

            def p_relu(p, k):
                if k == 0 and not (isinstance(p, int) and p == 0):
                    act.wait_ge(num_ps, TILES * p)
                act.activation((qT, kT)[k][:, :], psP[:, k, :], ACT.Relu, bias=bq[:, k:k + 1]).then_inc(k_relu if k else q_relu, 1)

            def p_kt(p):
                act.wait_ge(kt_ps, p + 1)
                act.activation(kt[:, :, :].rearrange("p t d -> p (t d)"), psP[:, 0, :], ACT.Copy).then_inc(kt_ready, 1)

            def a_norm2(s):
                act.wait_ge(shift_done["x1"], s + 1)
                normalise(un, x1, "x1", 1).then_inc(u2b_ready, 1)

            def a_norm3(s):
                act.wait_ge(shift_done["X"], s + 1)
                normalise(un, X, "X", 1).then_inc(u3b_ready, 1)

            def a_u2hi(s):
                act.wait_ge(u2T_ps, 2 * s + 1)
                act.activation(u2T_h[:, 0, :], psR[:, 0, :], ACT.Copy).then_inc(u2hi, 1)

            def a_gelu(s, i):
                act.wait_ge(f1_ps, 2 * FC * s + i + 1)
                if i >= 2:
                    act.wait_ge(g_hi, 2 * FC * s + i - 1)
                    wait_glo(act, s, i - 2)
                act.activation(gf[:, i % 2, :], (psA, psB)[i % 2][:, :], ACT.Gelu,
                               bias=f1bias[:, i % FC:i % FC + 1]).then_inc(gelu_done, 1)

            def a_y2(s, q):
                act.wait_ge(f2_ps, 2 * FC * s + FC * q + FC)
                b = seq(s, q)
                act.activation(y2[:, q, :], psR[:, q, :], ACT.Identity, scale=modc[:, GA, bass.ds(b, 1)],
                               bias=gaf2b[:, bass.ds(b, 1)]).then_inc(y2_ready, 1)

            def a_h2(s, q):
                act.wait_ge(u3T_ps, 2 * s + q + 1)
                b = seq(s, q)
                act.activation(h2T[:, q, :], psR[:, q, :], ACT.Identity, scale=modc[:, CB, bass.ds(b, 1)],
                               bias=modc[:, SB, bass.ds(b, 1)]).then_inc(h2_ready, 1)

            def a_tanh(s):
                act.wait_ge(gate_ps, s + 1)
                act.activation(th[:, :, :].rearrange("p k e -> p (k e)"), psR[:, 0, 0:8 * E], ACT.Tanh,
                               scale=0.5).then_inc(tanh_done, 1)

            def a_combT(s):
                act.wait_ge(parts_ps, s + 1)
                act.activation(combT[:, :], psR[0:3 * E, 1, :].bitcast(BF16), ACT.Copy).then_inc(combT_ready, 1)

            def c_silu(c, n):
                uu = n % ALLU
                act.wait_ge(w1_ps, 2 * ALLU * c + n + 1)
                if uu < UNITS:
                    act.activation(g[:, n % 2, :], psA[:, :], ACT.Silu).then_inc(silu_done, 1)
                else:
                    act.activation(g[F:P, n % 2, :], psC[0:F, :], ACT.Silu).then_inc(silu_done, 1)

            def c_hi(c, n):
                act.wait_ge(hid_ready, 2 * ALLU * c + n + 1)
                rows = slice(0, P) if n % ALLU < UNITS else slice(F, P)
                act.activation(hid_h[rows, n % 3, :], hid[rows, n % 3, :], ACT.Copy).then_inc(hid_hi, 1)

            def c_y(c, q):
                act.wait_ge(w2_ps, 2 * ALLU * c + ALLU * q + ALLU)
                act.activation(y[:, :], psY[:, :], ACT.Copy,
                               scale=modc[:, GB, bass.ds(seq(c, q), 1)]).then_inc(y_ready, 1)

            for q in range(2):
                m_norm(0, q)
            for q in range(2):
                p_norm(0, q)
            for q in range(2):
                p_u1hi(0, q)
            act.wait_ge(s_weights, 1)
            for q in range(2):
                m_norm(1, q)
            for k in range(2):
                p_exp(0, k)
                p_relu(0, k)
            p_kt(0)

            def iteration(c, s, p, m):
                for n in range(2 * ALLU + 2):
                    if n == MLP_SLOT and s is not None:
                        if c is None:
                            act.wait_ge(s_weights, 2)
                        for i in range(2 * FC):
                            a_gelu(s, i)
                            if i == 1 and c is not None:
                                c_hi(c, n - 1)
                            if i == 6:
                                a_y2(s, 0)
                        if c is not None:
                            c_silu(c, n)
                        a_y2(s, 1)
                    else:
                        if c is not None and n == ALLU + 2:
                            c_y(c, 0)
                        hi_first = n % ALLU in (MLP_SLOT + 1, UNITS)
                        if c is not None and 1 <= n <= 2 * ALLU and hi_first:
                            c_hi(c, n - 1)
                        if c is not None and 1 <= n < 2 * ALLU:
                            c_silu(c, n)
                        if c is not None and 1 <= n <= 2 * ALLU and not hi_first and n != 5:
                            c_hi(c, n - 1)
                    if p is not None and n == 0:
                        p_norm(p, 0)
                    if p is not None and n == 1:
                        p_norm(p, 1)
                    if p is not None and n == 3:
                        p_u1hi(p, 0)
                        p_u1hi(p, 1)
                    if c is not None and n == 4:
                        c_hi(c, n)
                    if s is not None and n == 4:
                        a_norm2(s)
                    if s is not None and n == 5:
                        a_u2hi(s)
                    if p is not None and n == 5:
                        p_exp(p, 0)
                        p_exp(p, 1)
                    if p is not None and n == 7:
                        p_relu(p, 0)
                        p_relu(p, 1)
                    if m is not None and n == 8:
                        m_norm(m, 0)
                    if m is not None and n == 9:
                        m_norm(m, 1)
                    if s is not None and n == 10:
                        a_norm3(s)
                    if s is not None and n == 11:
                        a_h2(s, 0)
                        a_h2(s, 1)
                    if s is not None and n == 12:
                        a_tanh(s)
                    if p is not None and n == (17 if c is not None else 10):
                        p_kt(p)
                    if s is not None and n == 18:
                        c_silu(s, 0)
                        a_combT(s)
                if c is not None:
                    c_y(c, 1)

            iterations(act, iteration)

        @block.gpsimd
        def _(pool):
            pool.memset(expo[:, :], -0.5).then_inc(s_pool0, 1)
            pool.memset(minus[:, :], -1.0).then_inc(s_pool0, 1)
            pool.memset(eps[:, :], LN_EPS).then_inc(s_pool0, 1)
            pool.wait_ge(s_pool0, 3)

            def inv_std(name, s):
                pool.wait_ge(mv_done[name], s + 1)
                pool.tensor_tensor(ve[name][:, :], mv[name][:, :, 1], eps[:, :], ALU.add).then_inc(ve_done[name], 1)
                pool.tensor_tensor(negm[name][:, :], mv[name][:, :, 0], minus[:, :], ALU.mult).then_inc(negm_done[name], 1)
                pool.wait_ge(ve_done[name], s + 1)
                pool.tensor_tensor(rstd[name][:, :], ve[name][:, :], expo[:, :], ALU.pow).then_inc(rstd_done[name], 1)
                pool.wait_ge(negm_done[name], s + 1)
                pool.wait_ge(rstd_done[name], s + 1)
                pool.tensor_tensor(shift[name][:, :], negm[name][:, :], rstd[name][:, :], ALU.mult).then_inc(shift_done[name], 1)

            def modrow(r, s, q):
                row = modr[:, r, bass.ds(seq(s, q), 1), :]
                return row.to_broadcast([P, TILES, D])

            def m_scale(m, q):
                pool.wait_ge(u_ready, 2 * m + q + 1)
                pool.tensor_tensor(u[:, q, :, :], u[:, q, :, :], modrow(ROW_CA, m, q), ALU.mult).then_inc(u_scaled, 1)

            def m_shift(m, q, halves=None):
                pool.wait_ge(u_scaled, halves or 2 * m + q + 1)
                pool.tensor_tensor(h[:, q, :, :], u[:, q, :, :], modrow(ROW_SA, m, q), ALU.add).then_inc(h_ready, 1)

            def p_hb(s, p, q):
                if s is not None:
                    pool.wait_ge(x1_ready, TILES * s + TILES)
                pool.tensor_tensor(hb[:, q, :, :], h[:, q, :, :], wide(ob_row[:, :]), ALU.add).then_inc(hb_ready, 1)

            def a_gate_x1(s, q):
                pool.wait_ge(x1_ready, TILES * s + TILES)
                pool.tensor_tensor(xg[:, q, :, :], x1[:, q, :, :], modrow(ROW_GA, s, q), ALU.mult).then_inc(x1_gated, 1)

            def a_mix(s, q):
                pool.wait_ge(x1_gated, 2 * s + q + 1)
                pool.wait_ge(xb_in[q], 16 * s + 16)
                pool.tensor_tensor(xg[:, q, :, :], xg[:, q, :, :], xb[:, q, :, :], ALU.add).then_inc(xg_ready, 1)

            def a_glo(s, i):
                pool.wait_ge(g_hi, 2 * FC * s + i + 1)
                pool.tensor_tensor(glo[:, i % 3, :], gf[:, i % 2, :], ghi[:, i % 3, :].bitcast(F32),
                                   ALU.subtract).then_inc(g_lo_pool, 1)

            def a_h2lo(s, q):
                pool.wait_ge(h2hi, 2 * s + q + 1)
                pool.tensor_tensor(h2_l[:, q, :], h2T[:, q, :], h2_h[:, q, :].bitcast(F32), ALU.subtract).then_inc(h2lo, 1)

            def c_lo(c, n):
                pool.wait_ge(hid_hi, 2 * ALLU * c + n + 1)
                pool.tensor_tensor(hid_l[:, n % 3, :], hid[:, n % 3, :], hid_h[:, n % 3, :].bitcast(F32),
                                   ALU.subtract).then_inc(hid_lo, 1)

            inv_std("x", 0)
            pool.wait_ge(s_modr, 1)
            m_scale(0, 0)
            m_shift(0, 0, halves=2)
            inv_std("h", 0)
            pool.wait_ge(attn_in, 16 * len(ATTN))
            for q in range(2):
                p_hb(None, 0, q)
            inv_std("x", 1)
            pool.wait_ge(u1_ready, 2)
            for q in range(2):
                m_scale(1, q)
                m_shift(1, q)
            inv_std("h", 1)

            def iteration(c, s, p, m):
                for n in range(2 * ALLU + 2):
                    if c is not None and 1 <= n <= 2 * ALLU:
                        c_lo(c, n - 1)
                    if s is not None and n == 4:
                        inv_std("x1", s)
                    if s is not None and n == 5:
                        if c is None:
                            pool.wait_ge(s_modr, NSEQ // 2 + 1)
                        a_gate_x1(s, 0)
                    if s is not None and n == MLP_SLOT:
                        a_mix(s, 0)
                        a_gate_x1(s, 1)
                        a_glo(s, 5)
                        a_mix(s, 1)
                    if p is not None and n == MLP_SLOT:
                        p_hb(s, p, 0)
                        p_hb(s, p, 1)
                    if m is not None and n == 7:
                        inv_std("x", m)
                    if s is not None and n == 9:
                        inv_std("X", s)
                    if m is not None and n == 10:
                        m_scale(m, 0)
                    if m is not None and n == 11:
                        m_shift(m, 0)
                    if m is not None and n == 12:
                        m_scale(m, 1)
                    if m is not None and n == 13:
                        m_shift(m, 1)
                    if s is not None and n == 16:
                        a_h2lo(s, 0)
                    if c is not None and n == 1:
                        a_h2lo(c, 1)
                if m is not None:
                    inv_std("h", m)

            iterations(pool, iteration)

        @block.vector
        def _(dve):
            link = [0]

            def chain(ins):
                link[0] += 1
                ins.then_inc(s_setup, 1)
                dve.wait_ge(s_setup, link[0])

            def bn(name, src, k):
                return dve.bn_stats(stats[name][:, k, :], src)

            def aggregate(name, s):
                stand_alone(dve, st_done[name], s + 1)
                for k in range(8):
                    last = dve.bn_aggr(mv[name][:, k, :], stats[name][:, k, :])
                last.then_inc(mv_done[name], 1)

            def normalise(dst, src, name, q):
                for t in range(TILES):
                    k = q * TILES + t
                    last = dve.tensor_scalar(dst[:, q, t, :], src[:, q, t, :], mv[name][:, k, 0:1],
                                             rstd[name][:, k:k + 1], ALU.subtract, ALU.mult)
                return last

            def m_stats(m, k):
                if k % TILES == 0:
                    dve.wait_ge(xa_in[k // TILES], 16 * m + 16)
                last = bn("x", xa[:, k // TILES, k % TILES, :], k)
                if k == 7:
                    last.then_inc(st_done["x"], 1)

            def p_stats(p, q, halves=None):
                dve.wait_ge(h_ready, halves or 2 * p + q + 1)
                for t in range(TILES):
                    last = bn("h", h[:, q, t, :], q * TILES + t)
                if q:
                    last.then_inc(st_done["h"], 1)
                    aggregate("h", p)

            def p_u1lo(p, q):
                dve.wait_ge(u1hi, 2 * p + q + 1)
                dve.tensor_tensor(u1T_l[:, q, :], psP[:, q, :], u1T_h[:, q, :].bitcast(F32), ALU.subtract).then_inc(u1lo, 1)

            def p_v(p, q):
                dve.wait_ge(v_ps, 2 * p + q + 1)
                dve.tensor_tensor(v1[:, q, :, 0:D], psP[:, q, :].rearrange("p (t d) -> p t d", t=TILES),
                                  wide(vb_row[:, :]), ALU.add).then_inc(v_ready, 1)

            def p_elu(p, k):
                dve.wait_ge(k_relu if k else q_relu, p + 1)
                dve.scalar_tensor_tensor(out=(qT, kT)[k][:, :], in0=(eQ, eK)[k].rearrange("p t d -> p (t d)"), scalar=1.0,
                                         in1=(qT, kT)[k][:, :], op0=ALU.min, op1=ALU.add).then_inc(kT_ready if k else qT_ready, 1)

            def a_mask(s, t):
                dve.wait_ge(sc_ps, TILES * s + t + 1)
                if t >= 2:
                    dve.wait_ge(num_ps, TILES * s + t - 1)
                dve.tensor_tensor(scT[:, t % 2, :, :], scores, wide(causal[:, :], 2), ALU.mult).then_inc(sc_ready, 1)

            def a_x1(s, t):
                n = TILES * s + t + 1
                if t == 0:
                    dve.wait_ge(hb_ready, 2 * s + 2)
                    dve.wait_ge(state_ready, s + 1)
                dve.wait_ge(num_ps, n)
                if t:
                    dve.wait_ge(state_sum, n - 1)
                dve.tensor_tensor(state[:, :], state[:, :], kv, ALU.add).then_inc(state_sum, 1)
                dve.tensor_scalar(den[:, t % 2, :], nums[:, :, D], ATTN_EPS, None, ALU.add).then_inc(den_ready, 1)
                dve.wait_ge(den_ready, n)
                dve.reciprocal(rden[:, t % 2, :], den[:, t % 2, :]).then_inc(rden_ready, 1)
                dve.wait_ge(rden_ready, n)
                for q in range(2):
                    last = dve.scalar_tensor_tensor(out=x1[:, q, t, :], in0=nums[:, q, 0:D], scalar=rden[:, t % 2, q:q + 1],
                                                    in1=hb[:, q, t, :], op0=ALU.mult, op1=ALU.add)
                last.then_inc(x1_ready, 1)
                if t == TILES - 1:
                    dve.wait_ge(state_sum, n)
                    dve.tensor_scalar(state[:, :], state[:, :], carry[:, bass.ds(s, 1)], None, ALU.mult).then_inc(state_ready, 1)

            def a_x1stats(s, t):
                dve.wait_ge(x1_ready, TILES * s + t + 1)
                for q in range(2):
                    last = bn("x1", x1[:, q, t, :], q * TILES + t)
                if t == TILES - 1:
                    last.then_inc(st_done["x1"], 1)

            def a_norm2(s):
                dve.wait_ge(rstd_done["x1"], s + 1)
                normalise(un, x1, "x1", 0).then_inc(u2_ready, 1)

            def a_u2hi(s):
                dve.wait_ge(u2T_ps, 2 * s + 2)
                dve.tensor_copy(u2T_h[:, 1, :], psR[:, 1, :]).then_inc(u2hi_dve, 1)

            def a_u2lo(s, q):
                dve.wait_ge(u2hi_dve if q else u2hi, s + 1)
                dve.tensor_tensor(u2T_l[:, q, :], psR[:, q, :], u2T_h[:, q, :].bitcast(F32), ALU.subtract).then_inc(u2lo, 1)

            def a_ghi(s, i):
                dve.wait_ge(gelu_done, 2 * FC * s + i + 1)
                dve.tensor_copy(ghi[:, i % 3, :], gf[:, i % 2, :]).then_inc(g_hi, 1)
                if i not in GLO_POOL:
                    dve.wait_ge(g_hi, 2 * FC * s + i + 1)
                    dve.tensor_tensor(glo[:, i % 3, :], gf[:, i % 2, :], ghi[:, i % 3, :].bitcast(F32),
                                      ALU.subtract).then_inc(g_lo_dve, 1)

            def a_X(s, q):
                dve.wait_ge(y2T_ps, 2 * s + q + 1)
                dve.wait_ge(xg_ready, 2 * s + q + 1)
                if q == 0 and not (isinstance(s, int) and s == 0):
                    dve.wait_ge(Xo_ready, 16 * s)
                dve.tensor_tensor(X[:, q, :, :], psR[:, q, :].rearrange("p (t d) -> p t d", t=TILES), xg[:, q, :, :],
                                  ALU.add).then_inc(X_ready, 1)

            def a_stats3(s, q):
                dve.wait_ge(X_ready, 2 * s + q + 1)
                for t in range(TILES):
                    last = bn("X", X[:, q, t, :], q * TILES + t)
                if q:
                    last.then_inc(st_done["X"], 1)

            def a_norm3(s):
                dve.wait_ge(rstd_done["X"], s + 1)
                normalise(un, X, "X", 0).then_inc(u3_ready, 1)

            def a_h2hi(s, q):
                dve.wait_ge(h2_ready, 2 * s + q + 1)
                dve.tensor_copy(h2_h[:, q, :], h2T[:, q, :]).then_inc(h2hi, 1)

            def a_route(s, link):
                if link == 0:
                    dve.wait_ge(tanh_done, s + 1)
                else:
                    stand_alone(dve, route, ROUTE * s + link)
                gm = gmax[:, :].rearrange("p (k g) -> p k g", g=NG)
                other = gm.unsqueeze(2).to_broadcast([P, 8, NG, NG])
                own = gm.unsqueeze(3).to_broadcast([P, 8, NG, NG])
                low = lower[:, :].unsqueeze(1).to_broadcast([P, 8, NG * NG])
                ge_f = ge[:, :, :, :].rearrange("p k g e -> p k (g e)")
                gt_f = gt[:, :, :, :].rearrange("p k g e -> p k (g e)")
                if link == 0:
                    dve.tensor_scalar(score[:, :, :], th[:, :, :], 0.5, 0.5, ALU.mult, ALU.add)
                    last = dve.scalar_tensor_tensor(out=biased[:, :, :], in0=th[:, :, :], scalar=0.5, in1=wide(gb_row[:, :], 8),
                                                    op0=ALU.mult, op1=ALU.add)
                elif link == 1:
                    last = dve.tensor_reduce(gmax[:, :], biased[:, :, :].rearrange("p k (g e) -> p (k g) e", g=NG), AX.X, ALU.max)
                elif link == 2:
                    dve.tensor_tensor(gt[:, :, :, :], other, own, ALU.is_gt)
                    last = dve.tensor_tensor(ge[:, :, :, :], other, own, ALU.is_ge)
                elif link == 3:
                    last = dve.tensor_tensor(ge_f, ge_f, low, ALU.mult)
                elif link == 4:
                    last = dve.tensor_tensor(gt_f, gt_f, ge_f, ALU.max)
                elif link == 5:
                    last = dve.tensor_reduce(rank[:, :], gt[:, :, :, :].rearrange("p k g e -> p (k g) e"), AX.X, ALU.add)
                elif link == 6:
                    last = dve.tensor_scalar(penalty[:, :, :].rearrange("p k g -> p (k g)"), rank[:, :], 1.5, MASKED,
                                             ALU.is_ge, ALU.mult)
                elif link == 7:
                    pen = penalty[:, :, :].unsqueeze(3).to_broadcast([P, 8, NG, E // NG])
                    last = dve.tensor_tensor(cand[:, :, 0:E].rearrange("p k (g e) -> p k g e", g=NG),
                                             biased[:, :, :].rearrange("p k (g e) -> p k g e", g=NG), pen, ALU.add)
                elif link == 8:
                    for k in range(8):
                        last = dve.max(top[:, k, :], cand[:, k, 0:E])
                elif link == 9:
                    last = dve.memset(top[:, :, 4:8], SENTINEL)
                elif link == 10:
                    for k in range(8):
                        last = dve.match_replace(marked[:, k, :], top[:, k, :], cand[:, k, :], CHOSEN)
                elif link == 11:
                    for dst in (comb[:, :, :], parts[:, :, 0:E]):
                        last = dve.scalar_tensor_tensor(out=dst, in0=marked[:, :, 0:E], scalar=CHOSEN / 2,
                                                        in1=score[:, :, :], op0=ALU.is_ge, op1=ALU.mult)
                elif link == 12:
                    for dst in (rest[:, :, :], parts[:, :, E:2 * E]):
                        last = dve.tensor_tensor(dst, comb[:, :, :], parts[:, :, 0:E], ALU.subtract)
                else:
                    last = dve.tensor_tensor(parts[:, :, 2 * E:3 * E], rest[:, :, :], parts[:, :, E:2 * E], ALU.subtract)
                    last.then_inc(parts_ready, 1)
                    return
                last.then_inc(route, 1)

            def c_gu(c, n):
                q, uu = n // ALLU, n % ALLU
                dve.wait_ge(silu_done, 2 * ALLU * c + n + 1)
                if uu == UNITS:
                    dve.tensor_tensor(hid[F:P, n % 3, :], psC[F:P, :], g[F:P, n % 2, :], ALU.mult).then_inc(hid_ready, 1)
                    return
                i = 2 * UNITS * c + UNITS * q + uu + 1
                dve.wait_ge(w3_ps, i)
                dve.tensor_tensor(gu[:, n % 2, :], psB[:, :], g[:, n % 2, :], ALU.mult).then_inc(gu_ready, 1)

            def c_hidden(c, n):
                q, uu = n // ALLU, n % ALLU
                if uu == UNITS:
                    return
                i = 2 * UNITS * c + UNITS * q + uu + 1
                dve.wait_ge(gu_ready, i)
                dve.wait_ge(comb_ps, i)
                dve.tensor_tensor(hid[:, n % 3, :], psC[:, :], gu[:, n % 2, :], ALU.mult).then_inc(hid_ready, 1)

            def c_out(c, q):
                dve.wait_ge(yT_ps, 2 * c + q + 1)
                dve.wait_ge(Xo_ready, 16 * c + 16)
                if isinstance(c, int) and c > 0:
                    dve.wait_ge(stored[q], 16 * c)
                dve.tensor_tensor(o[:, q, :, :], yT_of(q).rearrange("p (t d) -> p t d", t=TILES), Xo[:, q, :, :],
                                  ALU.add).then_inc(out_ready, 1)

            def split(hi, lo, src):
                chain(dve.tensor_copy(hi, src))
                return dve.tensor_tensor(lo, src, hi.bitcast(F32), ALU.subtract)

            def sign_of(v, sign):
                chain(dve.tensor_scalar(sign, v, 0.0, 2.0, ALU.is_ge, ALU.mult))
                chain(dve.tensor_scalar(sign, sign, 1.0, None, ALU.subtract))

            def clamp(v, sign):
                chain(dve.tensor_tensor(v, v, sign, ALU.mult))
                return dve.scalar_tensor_tensor(out=v, in0=v, scalar=0.25, in1=sign, op0=ALU.max, op1=ALU.mult)

            dve.memset(v1[:, :, :, D:D + 1], 1.0)
            dve.memset(cand[:, :, E:E + 4], SENTINEL)
            dve.memset(state[:, :], 0.0).then_inc(state_ready, 1)
            dve.wait_ge(s_silu, 1)
            dve.tensor_copy(flat(cspread).rearrange("p (b m) -> p b m", b=NSEQ),
                            silu_c[:, :].unsqueeze(2).to_broadcast([P, NSEQ, P])).then_inc(s_cb, 1)
            for k in range(8):
                m_stats(0, k)
            aggregate("x", 0)
            def modulation_rows(pair):
                for i in (2 * pair, 2 * pair + 1):
                    b = row_order[i]
                    dve.wait_ge(s_modr_ps, i + 1)
                    dve.tensor_copy(modr[:, :, b, :], banks[b][:, 0:3 * D].rearrange("p (r d) -> p r d", r=3)).then_inc(s_modr_cp, 1)
                dve.wait_ge(s_modr_cp, 2 * pair + 2)
                for b in row_order[2 * pair:2 * pair + 2]:
                    last = dve.tensor_scalar(modr[:, ROW_CA, b, :], modr[:, ROW_CA, b, :], 1.0, None, ALU.add)
                last.then_inc(s_modr, 1)

            for pair in range(NSEQ // 2 - 1):
                modulation_rows(pair)
            modrow = lambda r: modr[:, r, NSEQ // 2:NSEQ // 2 + 1, :].to_broadcast([P, TILES, D])
            dve.wait_ge(s_modr, 1)
            dve.wait_ge(u_ready, 2)
            dve.tensor_tensor(u[:, 1, :, :], u[:, 1, :, :], modrow(ROW_CA), ALU.mult).then_inc(u_scaled, 1)
            dve.wait_ge(u_scaled, 2)
            dve.tensor_tensor(h[:, 1, :, :], u[:, 1, :, :], modrow(ROW_SA), ALU.add).then_inc(h_ready, 1)
            modulation_rows(NSEQ // 2 - 1)
            for q in range(2):
                p_stats(0, q, halves=2)
            for k in range(8):
                m_stats(1, k)
            aggregate("x", 1)
            dve.wait_ge(small_in, 16 * len(SMALL))
            dve.wait_ge(s_fold_ps, 1)
            chain(dve.tensor_copy(wvo, psB[:, 0:D]))
            dve.tensor_copy(ln1b_sp, vecs[:, LN1B:LN1B + 1].to_broadcast([P, P]))
            dve.tensor_copy(vb_sp, vecs[:, VB:VB + 1].to_broadcast([P, P])).then_inc(s_wvo, 1)
            dve.wait_ge(s_modc_ps, 1)
            dve.tensor_tensor(bq[:, :], psC[:, 0:2], vecs[:, QB:QB + 2], ALU.add)
            dve.tensor_tensor(f1bias[:, :], psY[:, 0:FC], f1b[:, :], ALU.add)
            chain(dve.tensor_copy(modc[:, :, :], psA[:, 0:4 * NSEQ].rearrange("p (j b) -> p j b", j=4)))
            dve.wait_ge(attn_in, 16 * len(ATTN))
            dve.tensor_scalar(gb_row[:, :], gb_row[:, :], 0.5, None, ALU.add)
            qk = raw_qk[:, :]
            chain(dve.tensor_scalar(qk, qk, vecs[:, LN1W:LN1W + 1], None, ALU.mult))
            split(wqk_h[:, :, :].rearrange("p a b -> p (a b)"), wqk_l[:, :, :].rearrange("p a b -> p (a b)"), qk)
            dve.wait_ge(s_vb_ps, 1)
            chain(dve.tensor_copy(vb_row[:, :], psR[:, 0, 0:D]))
            chain(dve.tensor_scalar(wvo, wvo, vecs[:, LN1W:LN1W + 1], None, ALU.mult))
            split(wv_h[:, :], wv_l[:, :], wvo).then_inc(s_weights, 1)

            def split_moe(hi, lo, src):
                return split(hi[:, 0:UNITS, :].rearrange("p a b -> p (a b)"), lo[:, 0:UNITS, :].rearrange("p a b -> p (a b)"), src)

            p_u1lo(0, 0)
            p_u1lo(0, 1)
            chain(dve.tensor_scalar(raw_f1[:, 0, :], raw_f1[:, 0, :], vecs[:, LN2W:LN2W + 1], None, ALU.mult))
            split(f1_h[:, :, :].rearrange("p a b -> p (a b)"), f1_l[:, :, :].rearrange("p a b -> p (a b)"), raw_f1[:, 0, :])
            chain(dve.tensor_scalar(modc[:, CB, :], modc[:, CB, :], 1.0, None, ALU.add))
            for gate in (GA, GB):
                sign_of(modc[:, gate, :], rank[:, 0:NSEQ])
                chain(clamp(modc[:, gate, :], rank[:, 0:NSEQ]))
            chain(dve.tensor_scalar(gaf2b[:, :], modc[:, GA, :], vecs[:, F2B:F2B + 1], None, ALU.mult))
            p_v(0, 0)
            dve.wait_ge(moe_in, 16 * len(MOE))
            split_moe(w1_h, w1_l, flat(raw_w1))
            p_v(0, 1)
            split_moe(w3_h, w3_l, flat(raw_w3))
            p_elu(0, 0)
            gate_a = modr[:, ROW_GA, :, :].rearrange("p b d -> p (b d)")
            p_elu(0, 1)
            sign_of(gate_a, flat(un))
            split(f2_h[:, :, :].rearrange("p a b -> p (a b)"), f2_l[:, :, :].rearrange("p a b -> p (a b)"), raw_f2[:, 0, :])
            split(w1_h[:, UNITS, :], w1_l[:, UNITS, :], raw_sh[:, 0, 0:P])
            split(w2_h[F:P, UNITS, :], w2_l[F:P, UNITS, :], raw_sh[F:P, 1, 0:P])
            a_mask(0, 0)
            a_mask(0, 1)
            clamp(gate_a, flat(un)).then_inc(s_modr, 1)

            def rest_of_setup(n):
                if n == 0:
                    for q in range(2):
                        p_stats(1, q)
                elif n == 1:
                    split_moe(w2_h, w2_l, raw_w2[:, :, :].rearrange("p a b -> p (a b)")).then_inc(s_weights, 1)

            route_slots = {13: (0, 3), 14: (3, 6), 15: (6, 9), 16: (9, 11), 17: (11, 14)}

            def iteration(c, s, p, m):
                for n in range(2 * ALLU + 2):
                    if n == MLP_SLOT and s is not None:
                        for i in range(2 * FC):
                            a_ghi(s, i)
                            if m is not None:
                                m_stats(m, i)
                    links = list(range(*route_slots.get(n, (0, 0)))) if s is not None else []
                    if n == 2 * ALLU - 1:
                        while len(links) > 1:
                            a_route(s, links.pop(0))
                    if c is not None and 1 <= n < 2 * ALLU:
                        c_gu(c, n)
                    if s is not None and n == 8:
                        a_stats3(s, 1)
                    if s is not None and n == 9:
                        aggregate("X", s)
                    if s is not None and 1 <= n < TILES - 1:
                        a_mask(s, n + 1)
                    if links:
                        a_route(s, links.pop(0))
                    if c is not None and 1 <= n < 2 * ALLU:
                        c_hidden(c, n)
                    for link in links:
                        a_route(s, link)
                    if m is not None and n == MLP_SLOT:
                        aggregate("x", m)
                    if p is not None and n == 3:
                        p_u1lo(p, 0)
                        p_u1lo(p, 1)
                    if s is not None and n < TILES:
                        a_x1(s, n)
                        a_x1stats(s, n)
                        if n == TILES - 1:
                            aggregate("x1", s)
                        if c is None:
                            rest_of_setup(n)
                    if p is not None and n == 4:
                        p_v(p, 0)
                        p_v(p, 1)
                    if s is not None and n == 4:
                        a_norm2(s)
                    if s is not None and n == 5:
                        a_u2lo(s, 0)
                        a_u2hi(s)
                        a_u2lo(s, 1)
                    if s is not None and n == 7:
                        a_X(s, 0)
                        a_X(s, 1)
                        a_stats3(s, 0)
                    if p is not None and n == (11 if c is not None else 9):
                        p_elu(p, 0)
                        p_elu(p, 1)
                    if s is not None and n == 10:
                        a_norm3(s)
                    if c is not None and n == 1:
                        a_h2hi(c, 1)
                    if s is not None and n == 12:
                        a_h2hi(s, 0)
                    if c is not None and n == 12:
                        c_out(c, 0)
                    if m is not None and n == 17:
                        p_stats(m, 0)
                    if p is not None and n == (18 if c is not None else 12):
                        a_mask(p, 0)
                    if s is not None and n == 18:
                        c_gu(s, 0)
                    if m is not None and n == 18:
                        p_stats(m, 1)
                if p is not None:
                    a_mask(p, 1)
                if s is not None:
                    c_hidden(s, 0)
                if c is not None:
                    c_out(c, 1)

            iterations(dve, iteration)


def kernel(**inputs):
    import ml_dtypes
    import numpy as np

    import concourse.bacc as bacc
    from concourse.bass_utils import run_bass_kernel_spmd

    def get(name):
        return np.asarray(inputs["L0_" + name])

    qT, kT = get("attn_q_w").T, get("attn_k_w").T
    none = np.zeros_like(qT)
    two = lambda v: np.concatenate([v, v])
    vecs = [get("attn_ln1_w"), get("attn_ln1_b"), get("attn_ln2_w"), get("attn_ln2_b"), two(get("attn_q_b")),
            two(get("attn_k_b")), get("attn_v_b"), get("attn_f2_b")]
    chunks = lambda wT: wT.reshape(-1, P, wT.shape[1]).transpose(1, 0, 2).reshape(P, -1)
    w2 = get("ffn_w2").transpose(0, 2, 1).reshape(E * F, D)
    index = np.arange(P)
    group = np.arange(NG)
    spread = np.arange(3 * E)[:, None, None] % E == 2 * np.arange(UNITS)[:, None] + index // F
    arrays = {
        "x": get("attn_x").reshape(-1, D),
        "cT": get("c").T, "wmod": get("wmod"), "vecs": np.stack(vecs, axis=1),
        "f1b": get("attn_f1_b").reshape(FC, P).T,
        "v_w": get("attn_v_w"), "o_wT": get("attn_o_w").T,
        "qk_wT": np.concatenate([qT, none, none, qT, kT, none, none, kT], axis=1),
        "f1_wT": get("attn_f1_w").T, "f2_wT": chunks(get("attn_f2_w").T),
        "o_b": get("attn_o_b"), "gate_b": get("ffn_gate_bias"), "gate_wT": get("ffn_gate_w").T,
        "w1T": get("ffn_w1").reshape(E * F, D).T, "w3T": get("ffn_w3").reshape(E * F, D).T,
        "w2T": chunks(w2),
        "ws13T": np.concatenate([get("ffn_ws1").T, get("ffn_ws3").T], axis=1), "ws2T": get("ffn_ws2").T,
        "ident": np.eye(P, dtype=np.float32), "ident_b": np.eye(P, dtype=ml_dtypes.bfloat16),
        "causal": (index[:, None] <= index).astype(np.float32),
        "lower": np.tile((group < group[:, None]).astype(np.float32).reshape(1, -1), (P, 1)),
        "carry": np.tile((np.arange(STEPS) % 2 == 0).astype(np.float32), (P, 1)),
        "sel": spread.astype(ml_dtypes.bfloat16).reshape(3 * E, -1),
    }
    arrays = {n: np.ascontiguousarray(v) for n, v in arrays.items()}

    nc = bacc.Bacc("TRN2", target_bir_lowering=False, num_devices=1)
    a = {n: nc.dram_tensor(f"in_{n}", v.shape, mybir.dt.from_np(v.dtype), kind="ExternalInput").ap()
         for n, v in arrays.items()}
    a["o_b_row"] = a["o_b"].partition_broadcast(P)
    a["gate_b_row"] = a["gate_b"].partition_broadcast(P)
    a["out"] = nc.dram_tensor("out", arrays["x"].shape, F32, kind="ExternalOutput").ap()
    layer_kernel(nc, a)
    r = run_bass_kernel_spmd(nc, [{f"in_{n}": v for n, v in arrays.items()}], core_ids=[0])
    return r.results[0]["out"].reshape(inputs["L0_attn_x"].shape)
```
